# Optimizing a Trainium2 kernel written in Bass

```python
import numpy as np
import jax
import jax.numpy as jnp

def _softmax(x, axis=-1):
    return jax.nn.softmax(x, axis=axis)

def _gelu(x):
    return jax.nn.gelu(x, approximate=True)

def _silu(x):
    return jax.nn.silu(x)

def _sigmoid(x):
    return jax.nn.sigmoid(x)

def _layernorm(x, axis=-1, eps=1e-05):
    m = jnp.mean(x, axis=axis, keepdims=True)
    v = jnp.var(x, axis=axis, keepdims=True)
    return (x - m) / jnp.sqrt(v + eps)

def _scatter_add(tgt, idx, src, axis=0):
    return tgt.at[idx].add(src)

def _segment_sum(src, seg, n):
    return jax.ops.segment_sum(src, seg, n)
kernel_name = 'mk_adaln_d1_jaxref_r8_6022ec'

def setup_inputs(seed: int=0):
    np.random.seed(seed)
    _w = jnp.asarray

    def _L0_attn_setup():
        import jax, jax.numpy as jnp
        import numpy as np
        L, H, D, DH, DF = (4, 16, 128, 64, 512)
        B, S = (4, 128)

        def layer_norm(x, g, b):
            mu = jnp.mean(x, axis=-1, keepdims=True)
            var = jnp.mean((x - mu) ** 2, axis=-1, keepdims=True)
            return (x - mu) * jax.lax.rsqrt(var + 1e-05) * g + b

        def pos_encoding(seq_len, d):
            pos = jnp.arange(seq_len - 1, -1, -1, dtype=jnp.float32)
            freq = 1.0 / 10000.0 ** (jnp.arange(0, d, 2, dtype=jnp.float32) / d)
            ang = pos[:, None] * freq[None, :]
            return jnp.concatenate([jnp.sin(ang), jnp.cos(ang)], axis=-1)
        key = jax.random.key(seed)
        ks = jax.random.split(key, 16)
        s = 0.02
        return {'x': jax.random.normal(ks[0], (B, S, D), jnp.float32), 'W_qkv': jax.random.normal(ks[1], (L, D, 3 * H * DH), jnp.float32) * s, 'W_r': jax.random.normal(ks[2], (L, D, H * DH), jnp.float32) * s, 'W_o': jax.random.normal(ks[3], (L, H * DH, D), jnp.float32) * s, 'u': jax.random.normal(ks[4], (H, DH), jnp.float32) * s, 'v': jax.random.normal(ks[5], (H, DH), jnp.float32) * s, 'ln1_g': jnp.ones((L, D), jnp.float32), 'ln1_b': jnp.zeros((L, D), jnp.float32), 'W_ff1': jax.random.normal(ks[6], (L, D, DF), jnp.float32) * s, 'b_ff1': jnp.zeros((L, DF), jnp.float32), 'W_ff2': jax.random.normal(ks[7], (L, DF, D), jnp.float32) * s, 'b_ff2': jnp.zeros((L, D), jnp.float32), 'ln2_g': jnp.ones((L, D), jnp.float32), 'ln2_b': jnp.zeros((L, D), jnp.float32)}
    _L0_attn_in = _L0_attn_setup()

    def _L0_ffn_setup():
        import jax, jax.numpy as jnp
        import numpy as np
        B, S, H, F, E, K = (2, 256, 128, 512, 8, 2)

        def _init_w(key, shape, fan_in):
            return jax.random.normal(key, shape, jnp.float32) * fan_in ** (-0.5)

        def _ffn(x, wi, bi, wo, bo):
            return jax.nn.selu(x @ wi + bi) @ wo + bo
        key = jax.random.key(seed)
        ks = jax.random.split(key, 6)
        return {'x': jax.random.normal(ks[0], (B, S, H), jnp.float32), 'gate_wi': _init_w(ks[1], (H, F), H), 'gate_bi': jnp.zeros((F,), jnp.float32), 'gate_wo': _init_w(ks[2], (F, H), F), 'gate_bo': jnp.zeros((H,), jnp.float32), 'exp_wi': _init_w(ks[3], (E, H, F), H), 'exp_bi': jnp.zeros((E, F), jnp.float32), 'exp_wo': _init_w(ks[4], (E, F, H), F), 'exp_bo': jnp.zeros((E, H), jnp.float32)}
    _L0_ffn_in = _L0_ffn_setup()
    _L0_c = _w((lambda *s: np.random.randn(*s).astype(np.float32) * 0.05)(4, 128))
    _L0_wmod = _w((lambda *s: np.random.randn(*s).astype(np.float32) * 0.05)(128, 6 * 128) * 128 ** (-0.5))
    _d = {'L0_attn_x': _L0_attn_in['x'], 'L0_attn_W_qkv': _L0_attn_in['W_qkv'], 'L0_attn_W_r': _L0_attn_in['W_r'], 'L0_attn_W_o': _L0_attn_in['W_o'], 'L0_attn_u': _L0_attn_in['u'], 'L0_attn_v': _L0_attn_in['v'], 'L0_attn_ln1_g': _L0_attn_in['ln1_g'], 'L0_attn_ln1_b': _L0_attn_in['ln1_b'], 'L0_attn_W_ff1': _L0_attn_in['W_ff1'], 'L0_attn_b_ff1': _L0_attn_in['b_ff1'], 'L0_attn_W_ff2': _L0_attn_in['W_ff2'], 'L0_attn_b_ff2': _L0_attn_in['b_ff2'], 'L0_attn_ln2_g': _L0_attn_in['ln2_g'], 'L0_attn_ln2_b': _L0_attn_in['ln2_b'], 'L0_ffn_gate_wi': _L0_ffn_in['gate_wi'], 'L0_ffn_gate_bi': _L0_ffn_in['gate_bi'], 'L0_ffn_gate_wo': _L0_ffn_in['gate_wo'], 'L0_ffn_gate_bo': _L0_ffn_in['gate_bo'], 'L0_ffn_exp_wi': _L0_ffn_in['exp_wi'], 'L0_ffn_exp_bi': _L0_ffn_in['exp_bi'], 'L0_ffn_exp_wo': _L0_ffn_in['exp_wo'], 'L0_ffn_exp_bo': _L0_ffn_in['exp_bo'], 'L0_c': _L0_c, 'L0_wmod': _L0_wmod}
    _x0 = _d['L0_attn_x']
    _d['L0_attn_x'] = jax.random.normal(jax.random.fold_in(jax.random.key(seed), 1), (4, 512, 128), dtype=_x0.dtype)
    del _x0
    return _d

def reference(L0_attn_x, L0_attn_W_qkv, L0_attn_W_r, L0_attn_W_o, L0_attn_u, L0_attn_v, L0_attn_ln1_g, L0_attn_ln1_b, L0_attn_W_ff1, L0_attn_b_ff1, L0_attn_W_ff2, L0_attn_b_ff2, L0_attn_ln2_g, L0_attn_ln2_b, L0_ffn_gate_wi, L0_ffn_gate_bi, L0_ffn_gate_wo, L0_ffn_gate_bo, L0_ffn_exp_wi, L0_ffn_exp_bi, L0_ffn_exp_wo, L0_ffn_exp_bo, L0_c, L0_wmod):

    def _L0_attn_ref(x, W_qkv, W_r, W_o, u, v, ln1_g, ln1_b, W_ff1, b_ff1, W_ff2, b_ff2, ln2_g, ln2_b):
        import jax, jax.numpy as jnp
        import numpy as np
        L, H, D, DH, DF = (4, 16, 128, 64, 512)
        B, S = (4, 128)

        def layer_norm(x, g, b):
            mu = jnp.mean(x, axis=-1, keepdims=True)
            var = jnp.mean((x - mu) ** 2, axis=-1, keepdims=True)
            return (x - mu) * jax.lax.rsqrt(var + 1e-05) * g + b

        def pos_encoding(seq_len, d):
            pos = jnp.arange(seq_len - 1, -1, -1, dtype=jnp.float32)
            freq = 1.0 / 10000.0 ** (jnp.arange(0, d, 2, dtype=jnp.float32) / d)
            ang = pos[:, None] * freq[None, :]
            return jnp.concatenate([jnp.sin(ang), jnp.cos(ang)], axis=-1)
        b, s_len, _ = x.shape
        r = pos_encoding(s_len, D)
        h = x
        inv_sqrt_d = 1.0 / jnp.sqrt(jnp.float32(DH))
        for i in range(L):
            qkv = h @ W_qkv[i]
            q, k, val = jnp.split(qkv, 3, axis=-1)
            q = q.reshape(b, s_len, H, DH)
            k = k.reshape(b, s_len, H, DH)
            val = val.reshape(b, s_len, H, DH)
            kr = (r @ W_r[i]).reshape(s_len, H, DH)
            AC = jnp.einsum('bqhd,bkhd->bhqk', q + u, k)
            BD = jnp.einsum('bqhd,khd->bhqk', q + v, kr)
            prob = jax.nn.softmax((AC + BD) * inv_sqrt_d, axis=-1)
            vec = jnp.einsum('bhqk,bkhd->bqhd', prob, val).reshape(b, s_len, H * DH)
            h = layer_norm(h + vec @ W_o[i], ln1_g[i], ln1_b[i])
            ff = jax.nn.relu(h @ W_ff1[i] + b_ff1[i]) @ W_ff2[i] + b_ff2[i]
            h = layer_norm(ff, ln2_g[i], ln2_b[i])
        return h

    def _L0_ffn_ref(x, gate_wi, gate_bi, gate_wo, gate_bo, exp_wi, exp_bi, exp_wo, exp_bo):
        import jax, jax.numpy as jnp
        import numpy as np
        B, S, H, F, E, K = (2, 256, 128, 512, 8, 2)

        def _init_w(key, shape, fan_in):
            return jax.random.normal(key, shape, jnp.float32) * fan_in ** (-0.5)

        def _ffn(x, wi, bi, wo, bo):
            return jax.nn.selu(x @ wi + bi) @ wo + bo
        Bb, Ss, Hh = x.shape
        xf = x.reshape(-1, Hh)
        gate_logits = _ffn(xf, gate_wi, gate_bi, gate_wo, gate_bo)
        topv, topi = jax.lax.top_k(gate_logits, K)
        topv = topv / jnp.sum(topv, axis=-1, keepdims=True)
        onehot = (topi[..., None] == jnp.arange(E)).astype(x.dtype)
        w = jnp.einsum('nk,nke->ne', topv, onehot)
        h = jax.nn.selu(jnp.einsum('nh,ehf->enf', xf, exp_wi) + exp_bi[:, None, :])
        out_e = jnp.einsum('enf,efh->enh', h, exp_wo) + exp_bo[:, None, :]
        out = jnp.einsum('enh,ne->nh', out_e, w)
        return out.reshape(Bb, Ss, Hh)
    x = L0_attn_x
    mod = (_silu(L0_c) @ L0_wmod).reshape(L0_c.shape[0], 6, 1, -1)
    sa, ca, ga, sb, cb, gb = (mod[:, 0], mod[:, 1], mod[:, 2], mod[:, 3], mod[:, 4], mod[:, 5])
    ga = (2 * (ga >= 0) - 1) * jnp.maximum(jnp.abs(ga), 0.25)
    gb = (2 * (gb >= 0) - 1) * jnp.maximum(jnp.abs(gb), 0.25)
    h = _layernorm(x, axis=-1) * (1 + ca) + sa
    x = x + ga * _L0_attn_ref(h, L0_attn_W_qkv, L0_attn_W_r, L0_attn_W_o, L0_attn_u, L0_attn_v, L0_attn_ln1_g, L0_attn_ln1_b, L0_attn_W_ff1, L0_attn_b_ff1, L0_attn_W_ff2, L0_attn_b_ff2, L0_attn_ln2_g, L0_attn_ln2_b)
    h = _layernorm(x, axis=-1) * (1 + cb) + sb
    x = x + gb * _L0_ffn_ref(h, L0_ffn_gate_wi, L0_ffn_gate_bi, L0_ffn_gate_wo, L0_ffn_gate_bo, L0_ffn_exp_wi, L0_ffn_exp_bi, L0_ffn_exp_wo, L0_ffn_exp_bo)
    return x

_drawn_inputs = setup_inputs


def setup_inputs(seed=0):
    import zlib

    import numpy as np

    out = dict(_drawn_inputs(seed))
    spreads = {'L0_attn_ln1_g': (1.0, 0.2),
     'L0_attn_ln1_b': (0.0, 0.386),
     'L0_attn_b_ff1': (0.0, 0.1),
     'L0_attn_b_ff2': (0.0, 0.1),
     'L0_attn_ln2_g': (1.0, 0.2),
     'L0_attn_ln2_b': (0.0, 0.269),
     'L0_ffn_gate_bi': (0.0, 0.336),
     'L0_ffn_gate_bo': (0.0, 0.488),
     'L0_ffn_exp_bi': (0.0, 0.8),
     'L0_ffn_exp_bo': (0.0, 0.8)}
    factors = {'L0_attn_W_r': 8.0, 'L0_attn_u': 8.0, 'L0_attn_v': 8.0}
    for name, (base, spread) in spreads.items():
        noise = np.random.default_rng([zlib.crc32(name.encode()), seed]).standard_normal(out[name].shape)
        drawn = base * np.exp(spread * noise) if base else spread * noise
        out[name] = jnp.asarray(drawn.astype(out[name].dtype))
    for name, factor in factors.items():
        out[name] = (out[name] * factor).astype(out[name].dtype)
    return out
```

```python
from contextlib import ExitStack

import numpy as np

import concourse.bass as bass
from concourse import mybir

F32 = mybir.dt.float32
U32 = mybir.dt.uint32
ALU = mybir.AluOpType
ACT = mybir.ActivationFunctionType
AX_X = mybir.AxisListType.X

P = 128
EPS = 1e-5
SELU_SCALE = 1.0507009873554805
SELU_ALPHA = 1.6732632423543772


def wait_alone(engine, signal, value):
    engine.wait_ge(signal, value)
    engine.nop(nofuse=True)


def adaln_block(nc, x_d, wqkv_d, wr_d, wo_d, u_d, v_d, ln1g_d, ln1b_d, wf1_d, bf1_d, wf2_d, bf2_d, ln2g_d, ln2b_d,
                gwi_d, gbi_d, gwo_d, gbo_d, ewi_d, ebi_d, ewo_d, ebo_d, c_d, wmod_d, rt_d, out_d):
    B, S, D = x_d.shape
    L, _, QKV = wqkv_d.shape
    HD = QKV // 3
    DH = 64
    PAIRS = HD // P
    DF = wf1_d.shape[2]
    FT = DF // P
    E = ewi_d.shape[0]
    KT = S // P
    NT = B * KT
    STEPS = PAIRS * 2 * KT
    QS = DH ** -0.5
    TPP = 2 * KT
    FILLS = 3 * PAIRS
    UNITS = E + 1
    LNP = 5
    LOADS_Q, LOADS_O = 2, 8

    ctx = ExitStack()
    with ctx:
        def sb(name, shape, dt=F32):
            return ctx.enter_context(nc.sbuf_tensor(name, shape, dt))

        def ps(name):
            return ctx.enter_context(nc.psum_tensor(name, [P, 512], F32))

        def sem(name):
            return ctx.enter_context(nc.semaphore(name))

        X = sb("X", [P, NT * D])
        H = sb("H", [P, NT * D])
        HT = sb("HT", [P, B * S])
        HTC = sb("HTC", [P, S])
        MOD = sb("MOD", [P, B, 3 * D])
        CT = sb("CT", [P, B])
        CE = sb("CE", [P, B])
        CB = sb("CB", [P, B, P])
        WM = sb("WM", [P, 6 * D])
        WQKV = sb("WQKV", [P, QKV])
        WR = sb("WR", [P, HD])
        WO = sb("WO", [P, PAIRS, D])
        WF1 = sb("WF1", [P, DF])
        WF2 = sb("WF2", [P, FT, D])
        BF1 = sb("BF1", [P, FT])
        LN = sb("LN", [P, LNP, D])
        U = sb("U", [P, PAIRS])
        V_ = sb("V_", [P, PAIRS])
        RT = sb("RT", [P, S])
        ident = sb("ident", [P, P])
        Q = sb("Q", [P, 2, 2, S])
        K = sb("K", [P, 2 * PAIRS, S])
        VV = sb("VV", [P, 2, KT, P])
        PR = sb("PR", [P, 4, S])
        PT = sb("PT", [P, 2, 2, KT, S])
        VEC = sb("VEC", [P, PAIRS, S])
        F = sb("F", [P, FT, S])
        Y = sb("Y", [P, KT, D])
        Z = sb("Z", [P, KT, D])
        YT = sb("YT", [P, S])
        GWI = sb("GWI", [P, DF])
        GWO = sb("GWO", [P, FT, D])
        GBI = sb("GBI", [P, FT])
        EWI = sb("EWI", [P, E, DF])
        EBI = sb("EBI", [P, E, FT])
        GBO = sb("GBO", [P, D])
        EBO = sb("EBO", [P, E, D])
        ST = sb("ST", [P, NT, 6])
        MV = sb("MV", [P, NT, 2])
        VE = sb("VE", [P, NT])
        RS = sb("RS", [P, NT])
        HALF = sb("HALF", [P, NT])
        NMX = sb("NMX", [P, 8])
        SUM = sb("SUM", [P, 8])
        RC = sb("RC", [P, 8])
        EWO = VEC[:, :, :].rearrange("p a b -> p (a b)").rearrange("p (e f d) -> p e f d", e=E, f=FT)
        HID = PT[:, 0].rearrange("p a b c -> p (a b c)").rearrange("p (s f n) -> p s f n", s=2, f=FT)
        EX = PR
        RL = F
        ACC = Z
        TOP = sb("TOP", [P, KT, 8])
        TIX = sb("TIX", [P, KT, 8], U32)
        TIF = sb("TIF", [P, KT, 8])
        W12 = sb("W12", [P, KT, 2, E])
        WS = sb("WS", [P, KT, 2])
        WG = sb("WG", [P, KT, E])
        IOTA = sb("IOTA", [P, E])

        SB = [ps(f"SB{i}") for i in range(3)]
        TB = [ps(f"TB{i}") for i in range(2)]
        PVB = ps("PVB")
        PJ = [ps(f"PJ{i}") for i in range(2)]
        FB = [SB[0], SB[1], SB[2], PVB]

        ld_x, ld_c, ld_k, ld_moe, ld_ewo = (sem(n) for n in ("ld_x", "ld_c", "ld_k", "ld_moe", "ld_ewo"))
        ld_q = sem("ld_q")
        ld_o = sem("ld_o")
        ident_ok = sem("ident_ok")
        dve_ok = sem("dve_ok")
        var_ok, rstd_ok = sem("var_ok"), sem("rstd_ok")
        exp_c, cb_ok, mod_ok, mod_in = sem("exp_c"), sem("cb_ok"), sem("mod_ok"), sem("mod_in")
        norm_ok, tr_ok, tr_in = sem("norm_ok"), sem("tr_ok"), sem("tr_in")
        kr_ok, kr_in = sem("kr_ok"), sem("kr_in")
        uv_ok, htc_ok = sem("uv_ok"), sem("htc_ok")
        proj_ok, proj_in = sem("proj_ok"), sem("proj_in")
        score_ok, max_ok, exp_ok, rec_ok, prob_ok = (sem(n) for n in ("score_ok", "max_ok", "exp_ok", "rec_ok", "prob_ok"))
        pt_ok, pt_in, pv_ok, vec_in = sem("pt_ok"), sem("pt_in"), sem("pv_ok"), sem("vec_in")
        wo_ok, h1_ok, h1t_ok, h1t_in, ff1_ok, relu_a, relu_d, ff2_ok, h2_ok, h2t_ok, h2t_in = (
            sem(n) for n in ("wo_ok", "h1_ok", "h1t_ok", "h1t_in", "ff1_ok", "relu_a", "relu_d", "ff2_ok", "h2_ok",
                             "h2t_ok", "h2t_in"))
        e1_ok, ee_ok, er_ok, et_ok, eh_ok, e2_ok, ey_ok, fin_ok, st_out = (
            sem(n) for n in ("e1_ok", "ee_ok", "er_ok", "et_ok", "eh_ok", "e2_ok", "ey_ok", "fin_ok", "st_out"))

        block = ctx.enter_context(nc.Block())

        @block.sync
        def _(sp):
            xt = x_d.rearrange("b (t p) d -> p (b t) d", p=P)
            ot = out_d.rearrange("b (t p) d -> p b t d", p=P)
            sp.dma_start(X[:, :].rearrange("p (t d) -> p t d", d=D), xt).then_inc(ld_x, 16)
            sp.dma_start(CT[:, :], c_d).then_inc(ld_c, 16)
            sp.dma_start(WM[:, :], wmod_d).then_inc(ld_c, 16)

            def load_q(l):
                sp.dma_start(WR[:, :], wr_d[l]).then_inc(ld_q, 16)
                sp.dma_start(WQKV[:, :], wqkv_d[l]).then_inc(ld_q, 16)

            def load_o(l):
                sp.dma_start(WO[:, :, :], wo_d[l].rearrange("(a p) d -> p a d", p=P)).then_inc(ld_o, 16)
                sp.dma_start(WF1[:, :], wf1_d[l]).then_inc(ld_o, 16)
                sp.dma_start(WF2[:, :, :], wf2_d[l].rearrange("(a p) d -> p a d", p=P)).then_inc(ld_o, 16)
                sp.dma_start(BF1[:, :], bf1_d[l]).then_inc(ld_o, 16)
                for n, row in enumerate((ln1g_d, ln1b_d, ln2g_d, ln2b_d)):
                    sp.dma_start(LN[:, n, :], row[l].partition_broadcast(P)).then_inc(ld_o, 16)
                sp.dma_start(LN[:, 4, :], bf2_d[l].partition_broadcast(P)).then_inc(ld_o, 16)

            load_q(0)
            sp.dma_start(RT[:, :], rt_d).then_inc(ld_k, 16)
            sp.dma_start(U[:, :], u_d).then_inc(ld_k, 16)
            sp.dma_start(V_[:, :], v_d).then_inc(ld_k, 16)
            load_o(0)
            for dst, src in ((GWI[:, :], gwi_d), (GWO[:, :, :], gwo_d.rearrange("(a p) d -> p a d", p=P)),
                             (GBI[:, :], gbi_d), (EWI[:, :, :], ewi_d.rearrange("e p f -> p e f")),
                             (EBI[:, :, :], ebi_d), (GBO[:, :], gbo_d.partition_broadcast(P)),
                             (EBO[:, :, :], ebo_d.rearrange("e d -> (e d)").partition_broadcast(P).rearrange("p (e d) -> p e d", e=E))):
                sp.dma_start(dst, src).then_inc(ld_moe, 16)
            with sp.Fori(1, L) as l:
                wait_alone(sp, kr_ok, l * PAIRS)
                wait_alone(sp, proj_ok, l * (B * FILLS))
                load_q(l)
                wait_alone(sp, h2t_in, l * B + 1)
                load_o(l)
            sp.wait_ge(wo_ok, L * B)
            for e in range(E):
                sp.dma_start(EWO[:, e], ewo_d[e].rearrange("(a p) d -> p a d", p=P)).then_inc(ld_ewo, 16)
            for g in range(B):
                sp.wait_ge(fin_ok, g + 1)
                sp.dma_start(ot[:, g], X[:, g * S:(g + 1) * S].rearrange("p (t d) -> p t d", d=D)).then_inc(st_out, 16)
            sp.wait_ge(st_out, 16 * B)

        @block.gpsimd
        def _(pool):
            nc.gpsimd.memset(ident[:, :], 0.0).then_inc(ident_ok, 1)
            pool.wait_ge(ident_ok, 1)
            nc.gpsimd.affine_select(out=ident[:, :], in_=ident[:, :], compare_op=ALU.not_equal, fill=1.0, base=0,
                                    pattern=[[-1, P]], channel_multiplier=1).then_inc(ident_ok, 1)
            nc.gpsimd.iota(IOTA[:, :], [[1, E]], base=0, channel_multiplier=0,
                           allow_small_or_imprecise_dtypes=True).then_inc(ident_ok, 1)
            nc.gpsimd.memset(HALF[:, :], -0.5).then_inc(ident_ok, 1)
            pool.wait_ge(ident_ok, 4)

            def rstd(n, tiles):
                pool.wait_ge(var_ok, n)
                nc.gpsimd.tensor_tensor(RS[:, 0:tiles], VE[:, 0:tiles], HALF[:, 0:tiles], ALU.pow).then_inc(rstd_ok, 1)

            rstd(1, NT)
            with pool.Fori(0, L * B) as it:
                tiles = pool.snap(it * STEPS)
                for t in range(STEPS):
                    wait_alone(pool, rec_ok, tiles + (t + 1))
                    pr = PR[:, t % 4, :]
                    nc.gpsimd.tensor_scalar(pr, pr, RC[:, t % 8:t % 8 + 1], 1.0, ALU.mult, ALU.mult).then_inc(prob_ok, 1)
                rstd(it * 2 + 2, KT)
                rstd(it * 2 + 3, KT)
            rstd(2 * L * B + 2, NT)
            with pool.Fori(0, B) as g:
                tiles = pool.snap(g * (UNITS * FT))
                for j in range(UNITS * FT):
                    wait_alone(pool, ee_ok, tiles + (j + 1))
                    e = EX[:, j % 4, :]
                    nc.gpsimd.tensor_scalar(e, e, 1.0, -1.0, ALU.min, ALU.add).then_inc(et_ok, 1)

        @block.scalar
        def _(act):
            act.wait_ge(ld_c, 32)
            nc.scalar.activation(CE[:, :], CT[:, :], ACT.Exp, scale=-1.0).then_inc(exp_c, 1)
            act.wait_ge(uv_ok, 1)
            with act.Fori(0, L) as l:
                for p in range(PAIRS):
                    act.wait_ge(kr_ok, l * PAIRS + (p + 1))
                    bank = PJ[p % 2]
                    nc.scalar.copy(K[DH:P, 2 * p, :], bank[0:DH, :])
                    nc.scalar.copy(K[DH:P, 2 * p + 1, :], bank[DH:P, :]).then_inc(kr_in, 1)
                with act.Fori(0, B) as b:
                    it = act.snap(l * B + b)
                    tiles = act.snap(it * STEPS)
                    fills = act.snap(it * FILLS)

                    def take_q(p):
                        act.wait_ge(proj_ok, fills + (3 * p + 1))
                        bank = PJ[(3 * p) % 2]
                        for h in range(2):
                            src = bank[h * DH:(h + 1) * DH, :]
                            for r, bias in enumerate((U, V_)):
                                last = nc.scalar.activation(Q[r * DH:(r + 1) * DH, p % 2, h, :], src, ACT.Identity, scale=QS,
                                                            bias=bias[h * DH:(h + 1) * DH, p:p + 1])
                        last.then_inc(proj_in, 1)

                    def take_k(p):
                        act.wait_ge(proj_ok, fills + (3 * p + 2))
                        bank = PJ[(3 * p + 1) % 2]
                        nc.scalar.copy(K[0:DH, 2 * p, :], bank[0:DH, :])
                        nc.scalar.copy(K[0:DH, 2 * p + 1, :], bank[DH:P, :]).then_inc(proj_in, 1)

                    def take_v(p):
                        act.wait_ge(proj_ok, fills + (3 * p + 3))
                        nc.scalar.copy(VV[:, p % 2], PJ[(3 * p + 2) % 2][:, :].rearrange("p (t d) -> p t d", d=P)
                                       ).then_inc(proj_in, 1)

                    def take_vec(p):
                        act.wait_ge(pv_ok, it * PAIRS + (p + 1))
                        nc.scalar.copy(VEC[:, p, :], PVB[:, :]).then_inc(vec_in, 1)

                    take_q(0)
                    take_k(0)
                    take_v(0)
                    for t in range(STEPS):
                        act.wait_ge(max_ok, tiles + (t + 1))
                        if t >= 4:
                            act.wait_ge(pt_ok, tiles + (t - 3))
                        nc.scalar.activation(PR[:, t % 4, :], SB[t % 3][:, :], ACT.Exp, bias=NMX[:, t % 8:t % 8 + 1],
                                             accum_out=SUM[:, t % 8:t % 8 + 1]).then_inc(exp_ok, 1)
                        p, r = divmod(t, TPP)
                        if p + 1 < PAIRS:
                            if r == 1:
                                take_q(p + 1)
                            if r == 3:
                                take_k(p + 1)
                            if r == 6:
                                take_v(p + 1)
                        if r == 6 and p >= 1:
                            take_vec(p - 1)
                    take_vec(PAIRS - 1)
                    act.wait_ge(h1t_ok, it + 1)
                    nc.scalar.copy(YT[:, :], TB[0][:, :]).then_inc(h1t_in, 1)
                    act.wait_ge(ld_o, (l + 1) * (16 * 9))
                    for f in range(0, FT, 2):
                        act.wait_ge(ff1_ok, it * FT + (f + 1))
                        nc.scalar.activation(F[:, f, :], FB[f][:, :], ACT.Relu, bias=BF1[:, f:f + 1]).then_inc(relu_a, 1)
                    act.wait_ge(h2t_ok, it + 1)
                    nc.scalar.copy(HT[:, bass.ts(b, S)], TB[1][:, :]).then_inc(h2t_in, 1)
            act.wait_ge(ld_moe, 16 * 7)
            with act.Fori(0, B) as g:
                tiles = act.snap(g * (UNITS * FT))
                for j in range(UNITS * FT):
                    u, f = divmod(j, FT)
                    bias = GBI[:, f:f + 1] if u == 0 else EBI[:, u - 1, f:f + 1]
                    act.wait_ge(e1_ok, tiles + (j + 1))
                    if j >= 4:
                        act.wait_ge(eh_ok, tiles + (j - 3))
                    nc.scalar.activation(EX[:, j % 4, :], FB[j % 4][:, :], ACT.Exp, bias=bias).then_inc(ee_ok, 1)

        @block.vector
        def _(dve):
            v = nc.vector

            def norm_stats(src, tiles, link, n):
                for t in range(tiles):
                    last = v.bn_stats(ST[:, t, :], src[:, t * D:(t + 1) * D])
                link(last)
                for t in range(tiles):
                    last = v.bn_aggr(MV[:, t, :], ST[:, t, :])
                link(last)
                v.tensor_scalar(VE[:, 0:tiles], MV[:, 0:tiles, 1], EPS, None, ALU.add).then_inc(var_ok, 1)
                wait_alone(dve, rstd_ok, n)

            def normalise(dst, src, tiles, link):
                for t in range(tiles):
                    last = v.tensor_scalar(dst[:, t * D:(t + 1) * D], src[:, t * D:(t + 1) * D], MV[:, t, 0:1],
                                           RS[:, t:t + 1], ALU.subtract, ALU.mult)
                link(last)

            def row(ap):
                return ap.unsqueeze(1).to_broadcast([P, KT, D])

            def tk(ap):
                return ap.rearrange("p (t d) -> p t d", d=D)

            def chain(base):
                n = [0]

                def link(ins):
                    n[0] += 1
                    ins.then_inc(dve_ok, 1)
                    if isinstance(base, int):
                        dve.wait_ge(dve_ok, base + n[0])
                    else:
                        wait_alone(dve, dve_ok, base + n[0])
                return link, n

            link, n0 = chain(0)
            dve.wait_ge(exp_c, 1)
            link(v.tensor_scalar(CE[:, :], CE[:, :], 1.0, None, ALU.add))
            link(v.reciprocal(CE[:, :], CE[:, :]))
            link(v.tensor_tensor(CE[:, :], CE[:, :], CT[:, :], ALU.mult))
            v.tensor_copy(CB[:, :, :], CE[:, :].unsqueeze(2).to_broadcast([P, B, P])).then_inc(cb_ok, 1)

            dve.wait_ge(ld_k, 48)
            v.tensor_scalar(U[:, :], U[:, :], QS, None, ALU.mult)
            v.tensor_scalar(V_[:, :], V_[:, :], QS, None, ALU.mult).then_inc(uv_ok, 1)

            def take_mod(n):
                for b in range(B):
                    dve.wait_ge(mod_ok, n * B + b + 1)
                    last = v.tensor_copy(MOD[:, b, :], PJ[b % 2][:, 0:3 * D])
                    last.then_inc(mod_in, 1)
                dve.wait_ge(mod_in, (n + 1) * B)

            def modulated(n, link):
                norm_stats(X, NT, link, n)
                normalise(H, X, NT, link)
                for b in range(B):
                    h = tk(H[:, b * S:(b + 1) * S])
                    last = v.scalar_tensor_tensor(out=h, in0=row(MOD[:, b, D:2 * D]), scalar=1.0, in1=h,
                                                  op0=ALU.add, op1=ALU.mult)
                link(last)
                for b in range(B):
                    h = tk(H[:, b * S:(b + 1) * S])
                    v.tensor_tensor(h, h, row(MOD[:, b, 0:D]), ALU.add).then_inc(norm_ok, 1)

            def take_transposed(n):
                for b in range(B):
                    dve.wait_ge(tr_ok, n * B + b + 1)
                    v.tensor_copy(HT[:, b * S:(b + 1) * S], TB[b % 2][:, :]).then_inc(tr_in, 1)

            def signed_gate(link):
                g = MOD[:, :, 2 * D:3 * D]
                a, s = tk(Y[:, :, :].rearrange("p a b -> p (a b)")), tk(Z[:, :, :].rearrange("p a b -> p (a b)"))
                link(v.scalar_tensor_tensor(out=a, in0=g, scalar=-1.0, in1=g, op0=ALU.mult, op1=ALU.max))
                link(v.tensor_scalar(a, a, 0.25, None, ALU.max))
                link(v.tensor_scalar(s, g, 0.0, 2.0, ALU.is_ge, ALU.mult))
                link(v.scalar_tensor_tensor(out=g, in0=s, scalar=-1.0, in1=a, op0=ALU.add, op1=ALU.mult))

            take_mod(0)
            dve.wait_ge(ld_x, 16)
            modulated(1, link)
            take_transposed(0)
            dve.wait_ge(tr_in, B)
            dve.sem_inc(h2t_in, 1)
            signed_gate(link)
            before = n0[0]

            LINKS = 11
            with dve.Fori(0, L) as l:
                with dve.Fori(0, B) as b:
                    it = dve.snap(l * B + b)
                    tiles = dve.snap(it * STEPS)
                    links = dve.snap(it * LINKS + before)
                    link, n1 = chain(links)
                    wait_alone(dve, h2t_in, it + 1)
                    v.tensor_copy(HTC[:, :], HT[:, bass.ts(b, S)]).then_inc(htc_ok, 1)

                    def reciprocal(t):
                        dve.wait_ge(exp_ok, tiles + (t + 1))
                        v.reciprocal(RC[:, t % 8:t % 8 + 1], SUM[:, t % 8:t % 8 + 1]).then_inc(rec_ok, 1)

                    def take_pt(t):
                        p, r = divmod(t, TPP)
                        h, q = divmod(r, KT)
                        dve.wait_ge(pt_ok, tiles + (t + 1))
                        if p >= 2 and r == 0:
                            dve.wait_ge(pv_ok, it * PAIRS + (p - 1))
                        v.tensor_copy(PT[:, p % 2, h, :, q * P:(q + 1) * P],
                                      TB[t % 2][:, :].rearrange("p (t d) -> p t d", d=P)).then_inc(pt_in, 1)

                    for t in range(STEPS):
                        if t >= 1:
                            reciprocal(t - 1)
                        dve.wait_ge(score_ok, tiles + (t + 1))
                        v.tensor_reduce(NMX[:, t % 8:t % 8 + 1], SB[t % 3][:, :], AX_X, ALU.max, negate=True
                                        ).then_inc(max_ok, 1)
                        if t >= 2:
                            take_pt(t - 2)
                    reciprocal(STEPS - 1)
                    take_pt(STEPS - 2)
                    take_pt(STEPS - 1)

                    y, z = Y[:, :, :].rearrange("p a b -> p (a b)"), Z[:, :, :].rearrange("p a b -> p (a b)")
                    dve.wait_ge(wo_ok, it + 1)
                    link(v.tensor_tensor(y, PJ[0][:, :], H[:, bass.ts(b, S)], ALU.add))
                    norm_stats(y, KT, link, it * 2 + 2)
                    normalise(y, y, KT, link)
                    dve.wait_ge(ld_o, (l + 1) * (16 * 9))
                    link(v.tensor_tensor(tk(y), tk(y), row(LN[:, 0, :]), ALU.mult))
                    v.tensor_tensor(tk(y), tk(y), row(LN[:, 1, :]), ALU.add).then_inc(h1_ok, 1)
                    for f in range(1, FT, 2):
                        dve.wait_ge(ff1_ok, it * FT + (f + 1))
                        v.tensor_scalar(F[:, f, :], FB[f][:, :], BF1[:, f:f + 1], 0.0, ALU.add, ALU.max
                                        ).then_inc(relu_d, 1)
                    dve.wait_ge(ff2_ok, it + 1)
                    link(v.tensor_tensor(tk(z), tk(PJ[1][:, :]), row(LN[:, 4, :]), ALU.add))
                    norm_stats(z, KT, link, it * 2 + 3)
                    normalise(z, z, KT, link)
                    link(v.tensor_tensor(tk(z), tk(z), row(LN[:, 2, :]), ALU.mult))
                    link(v.tensor_tensor(tk(z), tk(z), row(LN[:, 3, :]), ALU.add))
                    v.tensor_copy(H[:, bass.ts(b, S)], z).then_inc(h2_ok, 1)
                    assert n1[0] == LINKS, n1
            dve.wait_ge(h2t_in, L * B + 1)
            link, n2 = chain(L * B * LINKS + before)

            def add_branch(x, branch, b):
                link(v.tensor_tensor(branch, branch, row(MOD[:, b, 2 * D:3 * D]), ALU.mult))
                return v.tensor_tensor(x, x, branch, ALU.add)

            for b in range(B):
                last = add_branch(tk(X[:, b * S:(b + 1) * S]), tk(H[:, b * S:(b + 1) * S]), b)
            link(last)
            take_mod(1)
            modulated(2 * L * B + 2, link)
            take_transposed(1)
            dve.wait_ge(tr_in, 2 * B)
            signed_gate(link)
            before2 = L * B * LINKS + before + n2[0]

            dve.wait_ge(ld_moe, 16 * 7)
            dve.wait_ge(ident_ok, 4)
            TILES = UNITS * FT
            y, acc = Y[:, :, :], ACC[:, :, :]
            GLINKS = 8 + UNITS - 1
            with dve.Fori(0, B) as g:
                tiles = dve.snap(g * TILES)
                links = dve.snap(g * GLINKS + before2)
                link, n3 = chain(links)

                def positive(j):
                    u, f = divmod(j, FT)
                    bias = GBI[:, f:f + 1] if u == 0 else EBI[:, u - 1, f:f + 1]
                    dve.wait_ge(ee_ok, tiles + (j + 1))
                    v.tensor_scalar(RL[:, j % 4, :], FB[j % 4][:, :], bias, 0.0, ALU.add, ALU.max).then_inc(er_ok, 1)

                def selu(j):
                    u, f = divmod(j, FT)
                    if u >= 2 and f == 0:
                        dve.wait_ge(e2_ok, g * UNITS + (u - 1))
                    dve.wait_ge(et_ok, tiles + (j + 1))
                    dve.wait_ge(er_ok, tiles + (j + 1))
                    v.scalar_tensor_tensor(out=HID[:, u % 2, f, :], in0=EX[:, j % 4, :], scalar=SELU_ALPHA,
                                           in1=RL[:, j % 4, :], op0=ALU.mult, op1=ALU.add).then_inc(eh_ok, 1)

                def top2():
                    for t in range(KT):
                        last = v.max(TOP[:, t, :], Y[:, t, :])
                    link(last)
                    for t in range(KT):
                        last = v.max_index(TIX[:, t, :], TOP[:, t, :], Y[:, t, :])
                    link(last)
                    v.tensor_copy(TIF[:, :, :], TIX[:, :, :])
                    link(v.tensor_tensor(WS[:, :, 0:1], TOP[:, :, 0:1], TOP[:, :, 1:2], ALU.add))
                    link(v.reciprocal(WS[:, :, 1:2], WS[:, :, 0:1]))
                    link(v.tensor_tensor(TOP[:, :, 0:2], TOP[:, :, 0:2], WS[:, :, 1:2].to_broadcast([P, KT, 2]), ALU.mult))
                    for t in range(KT):
                        for k in range(2):
                            last = v.tensor_scalar(W12[:, t, k, :], IOTA[:, :], TIF[:, t, k:k + 1], TOP[:, t, k:k + 1],
                                                   ALU.is_equal, ALU.mult)
                    link(last)
                    link(v.tensor_tensor(WG[:, :, :], W12[:, :, 0, :], W12[:, :, 1, :], ALU.add))

                def take_out(u):
                    dve.wait_ge(e2_ok, g * UNITS + (u + 1))
                    bias = GBO[:, :] if u == 0 else EBO[:, u - 1, :]
                    ins = v.scalar_tensor_tensor(out=y, in0=tk(PJ[u % 2][:, :]), scalar=SELU_SCALE, in1=row(bias),
                                                 op0=ALU.mult, op1=ALU.add)
                    ins.then_inc(ey_ok, 1)
                    wait_alone(dve, ey_ok, g * UNITS + (u + 1))
                    if u == 0:
                        top2()
                        return
                    for t in range(KT):
                        w = WG[:, t, u - 1:u]
                        if u == 1:
                            last = v.tensor_scalar(ACC[:, t, :], Y[:, t, :], w, None, ALU.mult)
                        else:
                            last = v.scalar_tensor_tensor(out=ACC[:, t, :], in0=Y[:, t, :], scalar=w,
                                                          in1=ACC[:, t, :], op0=ALU.mult, op1=ALU.add)
                    link(last)

                for j in range(TILES):
                    positive(j)
                    if j >= 1:
                        selu(j - 1)
                    if j % FT == FT - 1 and j >= 2 * FT - 1:
                        take_out(j // FT - 1)
                selu(TILES - 1)
                take_out(UNITS - 1)
                gate = MOD[:, :, :].rearrange("p b d -> p (b d)")[:, bass.ts(g * 3 + 2, D)]
                link(v.tensor_tensor(acc, acc, gate.unsqueeze(1).to_broadcast([P, KT, D]), ALU.mult))
                x = X[:, bass.ts(g, S)]
                v.tensor_tensor(x, x, ACC[:, :, :].rearrange("p a b -> p (a b)"), ALU.add).then_inc(fin_ok, 1)
                assert n3[0] == GLINKS, n3

        @block.tensor
        def _(pe):
            mm = nc.tensor.matmul

            def mod_rows(n):
                for b in range(B):
                    i = n * B + b
                    if i >= 2:
                        pe.wait_ge(mod_in, i - 1)
                    mm(PJ[b % 2][:, 0:3 * D], CB[:, b, :], WM[:, n * 3 * D:(n + 1) * 3 * D], start=True, stop=True
                       ).then_inc(mod_ok, 1)

            def transposes(bank, src, done):
                for t in range(KT):
                    last = nc.tensor.transpose(bank[:, t * P:(t + 1) * P], src[:, t * P:(t + 1) * P], ident[:, :])
                last.then_inc(done, 1)

            def transpose_all(n):
                for b in range(B):
                    pe.wait_ge(norm_ok, n * B + b + 1)
                    if b >= 2:
                        pe.wait_ge(tr_in, n * B + b - 1)
                    transposes(TB[b % 2], H[:, b * S:(b + 1) * S], tr_ok)

            pe.wait_ge(cb_ok, 1)
            pe.wait_ge(ld_c, 32)
            mod_rows(0)
            pe.wait_ge(ident_ok, 4)
            transpose_all(0)
            pe.wait_ge(ld_k, 48)
            pe.wait_ge(tr_in, B)
            with pe.Fori(0, L) as l:
                pe.wait_ge(ld_q, (l + 1) * (16 * LOADS_Q))
                for p in range(PAIRS):
                    if p >= 2:
                        pe.wait_ge(kr_in, l * PAIRS + (p - 1))
                    mm(PJ[p % 2][:, :], WR[:, p * P:(p + 1) * P], RT[:, :], start=True, stop=True).then_inc(kr_ok, 1)
                wait_alone(pe, kr_in, (l + 1) * PAIRS)
                with pe.Fori(0, B) as b:
                    it = pe.snap(l * B + b)
                    tiles = pe.snap(it * STEPS)
                    fills = pe.snap(it * FILLS)
                    pairs = pe.snap(it * PAIRS)
                    pe.wait_ge(htc_ok, it + 1)

                    def fill(p, part):
                        n = 3 * p + part
                        if n >= 2:
                            pe.wait_ge(proj_in, fills + (n - 1))
                        bank = PJ[n % 2]
                        w = WQKV[:, part * HD + p * P:part * HD + (p + 1) * P]
                        if part < 2:
                            last = mm(bank[:, :], w, HTC[:, :], start=True, stop=True)
                        else:
                            for k in range(KT):
                                last = mm(bank[:, k * P:(k + 1) * P], HTC[:, k * P:(k + 1) * P], w, start=True, stop=True)
                        last.then_inc(proj_ok, 1)

                    def score(t):
                        p, r = divmod(t, TPP)
                        h, q = divmod(r, KT)
                        if r == 0:
                            pe.wait_ge(proj_in, fills + (3 * p + 2))
                        if t >= 3:
                            pe.wait_ge(exp_ok, tiles + (t - 2))
                        mm(SB[t % 3][:, :], Q[:, p % 2, h, q * P:(q + 1) * P], K[:, 2 * p + h, :], start=True, stop=True
                           ).then_inc(score_ok, 1)

                    def turn(t):
                        pe.wait_ge(prob_ok, tiles + (t + 1))
                        if t >= 2:
                            pe.wait_ge(pt_in, tiles + (t - 1))
                        transposes(TB[t % 2], PR[:, t % 4, :], pt_ok)

                    def values(p, k):
                        if k == 0:
                            pe.wait_ge(proj_in, fills + (3 * p + 3))
                            pe.wait_ge(pt_in, tiles + (p + 1) * TPP)
                            if p >= 1:
                                pe.wait_ge(vec_in, pairs + p)
                        for h in range(2):
                            last = mm(PVB[h * DH:(h + 1) * DH, :], VV[:, p % 2, k, h * DH:(h + 1) * DH],
                                      PT[:, p % 2, h, k, :], start=(k == 0), stop=(k == KT - 1))
                        if k == KT - 1:
                            last.then_inc(pv_ok, 1)

                    for part in range(3):
                        fill(0, part)
                    for t in range(STEPS):
                        p, r = divmod(t, TPP)
                        score(t)
                        if t >= 2:
                            turn(t - 2)
                        if p + 1 < PAIRS and r in (1, 3, 6):
                            fill(p + 1, {1: 0, 3: 1, 6: 2}[r])
                        if p >= 1 and 2 <= r < 2 + KT:
                            values(p - 1, r - 2)
                    turn(STEPS - 2)
                    turn(STEPS - 1)
                    for k in range(KT):
                        values(PAIRS - 1, k)

                    pe.wait_ge(vec_in, pairs + PAIRS)
                    pe.wait_ge(ld_o, (l + 1) * (16 * 9))
                    for q in range(KT):
                        for p in range(PAIRS):
                            last = mm(PJ[0][:, q * P:(q + 1) * P], VEC[:, p, q * P:(q + 1) * P], WO[:, p, :],
                                      start=(p == 0), stop=(p == PAIRS - 1))
                    last.then_inc(wo_ok, 1)
                    pe.wait_ge(h1_ok, it + 1)
                    transposes(TB[0], Y[:, :, :].rearrange("p a b -> p (a b)"), h1t_ok)
                    pe.wait_ge(h1t_in, it + 1)
                    for f in range(FT):
                        mm(FB[f][:, :], WF1[:, f * P:(f + 1) * P], YT[:, :], start=True, stop=True).then_inc(ff1_ok, 1)
                    pe.wait_ge(relu_a, (it + 1) * (FT // 2))
                    pe.wait_ge(relu_d, (it + 1) * (FT // 2))
                    for q in range(KT):
                        for f in range(FT):
                            last = mm(PJ[1][:, q * P:(q + 1) * P], F[:, f, q * P:(q + 1) * P], WF2[:, f, :],
                                      start=(f == 0), stop=(f == FT - 1))
                    last.then_inc(ff2_ok, 1)
                    pe.wait_ge(h2_ok, it + 1)
                    transposes(TB[1], Z[:, :, :].rearrange("p a b -> p (a b)"), h2t_ok)

            pe.wait_ge(h2t_in, L * B + 1)
            mod_rows(1)
            transpose_all(1)
            pe.wait_ge(tr_in, 2 * B)
            pe.wait_ge(ld_moe, 16 * 7)
            pe.wait_ge(ld_ewo, 16 * E)
            TILES = UNITS * FT
            with pe.Fori(0, B) as g:
                tiles = pe.snap(g * TILES)

                def hidden(u):
                    for f in range(FT):
                        j = u * FT + f
                        if j >= 4:
                            pe.wait_ge(er_ok, tiles + (j - 3))
                        w = GWI[:, f * P:(f + 1) * P] if u == 0 else EWI[:, u - 1, f * P:(f + 1) * P]
                        mm(FB[j % 4][:, :], w, HT[:, bass.ts(g, S)], start=True, stop=True).then_inc(e1_ok, 1)

                def second(u):
                    pe.wait_ge(eh_ok, tiles + (u + 1) * FT)
                    if u >= 2:
                        pe.wait_ge(ey_ok, g * UNITS + (u - 1))
                    for q in range(KT):
                        for f in range(FT):
                            w = GWO[:, f, :] if u == 0 else EWO[:, u - 1, f, :]
                            last = mm(PJ[u % 2][:, q * P:(q + 1) * P], HID[:, u % 2, f, q * P:(q + 1) * P], w,
                                      start=(f == 0), stop=(f == FT - 1))
                    last.then_inc(e2_ok, 1)

                hidden(0)
                for u in range(UNITS):
                    if u + 1 < UNITS:
                        hidden(u + 1)
                    second(u)
                pe.wait_ge(fin_ok, g + 1)


def kernel(**inputs):
    import concourse.bacc as _bacc
    from concourse.bass_utils import run_bass_kernel_spmd as _run

    a = {k: np.asarray(x) for k, x in inputs.items()}
    B, S, D = a["L0_attn_x"].shape
    L = a["L0_attn_W_qkv"].shape[0]
    FT = a["L0_attn_b_ff1"].shape[1] // P
    E = a["L0_ffn_exp_bi"].shape[0]
    pos = np.arange(S - 1, -1, -1, dtype=np.float32)
    freq = (np.float32(1.0) / np.float32(10000.0) ** (np.arange(0, D, 2, dtype=np.float32) / np.float32(D))).astype(np.float32)
    ang = (pos[:, None] * freq[None, :]).astype(np.float32)
    enc = np.concatenate([np.sin(ang), np.cos(ang)], axis=-1).astype(np.float32)
    g = lambda n: a["L0_" + n]
    arrays = [
        g("attn_x"), g("attn_W_qkv"), g("attn_W_r"), g("attn_W_o"),
        g("attn_u").reshape(-1, P).T, g("attn_v").reshape(-1, P).T,
        g("attn_ln1_g"), g("attn_ln1_b"), g("attn_W_ff1"), g("attn_b_ff1").reshape(L, FT, P).transpose(0, 2, 1),
        g("attn_W_ff2"), g("attn_b_ff2"), g("attn_ln2_g"), g("attn_ln2_b"),
        g("ffn_gate_wi"), g("ffn_gate_bi").reshape(FT, P).T, g("ffn_gate_wo"), g("ffn_gate_bo"),
        g("ffn_exp_wi"), g("ffn_exp_bi").reshape(E, FT, P).transpose(2, 0, 1), g("ffn_exp_wo"), g("ffn_exp_bo"),
        g("c").T, g("wmod"), enc.T,
    ]
    nc = _bacc.Bacc("TRN2", target_bir_lowering=False, num_devices=1)
    sent, args = {}, []
    for i, x in enumerate(arrays):
        x = np.ascontiguousarray(x)
        sent[f"in_{i}"] = x
        args.append(nc.dram_tensor(f"in_{i}", x.shape, mybir.dt.from_np(x.dtype), kind="ExternalInput").ap())
    args.append(nc.dram_tensor("out", (B, S, D), F32, kind="ExternalOutput").ap())
    adaln_block(nc, *args)
    r = _run(nc, [sent], core_ids=[0])
    return r.results[0]["out"]
```

```python
from contextlib import ExitStack

import numpy as np

import concourse.bass as bass
from concourse import mybir

F32 = mybir.dt.float32
F32R = mybir.dt.float32r
U32 = mybir.dt.uint32
ALU = mybir.AluOpType
ACT = mybir.ActivationFunctionType
AX_X = mybir.AxisListType.X

P = 128
EPS = 1e-5
SELU_SCALE = 1.0507009873554805
SELU_ALPHA = 1.6732632423543772


def wait_alone(engine, signal, value):
    engine.wait_ge(signal, value)
    engine.nop(nofuse=True)


def places(fills, first_bank):
    on, found = [0, 0], {}
    for n, key in enumerate(fills):
        bank = (n + first_bank) % 2
        on[bank] += 1
        found[key] = (n + 1, bank, on[bank])
    return found, on


def adaln_block(nc, x_d, wqkv_d, wr_d, wo_d, u_d, v_d, ln1g_d, ln1b_d, wf1_d, bf1_d, wf2_d, bf2_d, ln2g_d, ln2b_d,
                gwi_d, gbi_d, gwo_d, gbo_d, ewi_d, ebi_d, ewo_d, ebo_d, c_d, wmod_d, rt_d, out_d):
    B, S, D = x_d.shape
    L, _, QKV = wqkv_d.shape
    HD = QKV // 3
    DH = 64
    PAIRS = HD // P
    DF = wf1_d.shape[2]
    FT = DF // P
    E = ewi_d.shape[0]
    KT = S // P
    NT = B * KT
    STEPS = PAIRS * 2 * KT
    QS = DH ** -0.5
    TPP = 2 * KT

    LAST = PAIRS - 1
    fill_at = {("o", 0): 4, ("h1", 0): 13, ("f2", 0): 23, ("h2", 0): 35}
    fill_at |= {("f1", f): t for f, t in enumerate((15, 16, 19, 20))}
    for p in range(PAIRS):
        fill_at |= {("q", p + 1): p * TPP + 1, ("k", p + 1): p * TPP + 2, ("v", p + 1): p * TPP + 6}
    fill_at["v", PAIRS] = STEPS
    at_step = {t: key for key, t in fill_at.items()}
    Y_AT, Z_AT, HTC_AT = 6, 25, LAST * TPP - 1
    PROLOGUE, PRO_ON = places([("kr", p) for p in range(PAIRS)] + [("c", 0)] + [("q", 0), ("k", 0), ("v", 0)], 0)
    BODY, BODY_ON = places(sorted(fill_at, key=fill_at.get), len(PROLOGUE) % 2)
    END, END_ON = places([("o", 0), ("h1", 0)] + [("f1", f) for f in range(FT)] + [("f2", 0), ("h2", 0)], 0)
    LAYER_FILLS = len(PROLOGUE) + B * len(BODY)
    LAYER_ON = [PRO_ON[k] + B * BODY_ON[k] for k in range(2)]
    assert len(at_step) == len(fill_at) and L & (L - 1) == 0 and B & (B - 1) == 0
    UNITS = E + 1
    LNP = 5
    LOADS_Q, LOADS_O = 2, 9
    HEADS = 2 * PAIRS
    CS = 4
    LAYER_PAIRS = 1 + B * PAIRS

    ctx = ExitStack()
    with ctx:
        def sb(name, shape, dt=F32):
            return ctx.enter_context(nc.sbuf_tensor(name, shape, dt))

        def ps(name):
            return ctx.enter_context(nc.psum_tensor(name, [P, 512], F32))

        def sem(name):
            return ctx.enter_context(nc.semaphore(name))

        X = sb("X", [P, NT * D])
        H = sb("H", [P, (B + 1) * KT * D])
        HT = sb("HT", [P, (B + 1) * S])
        HTC = sb("HTC", [P, S])
        MOD = sb("MOD", [P, B, 3 * D])
        CT = sb("CT", [P, B])
        CE = sb("CE", [P, B])
        CB = sb("CB", [P, B, P])
        WM = sb("WM", [P, 6 * D])
        WQKV = sb("WQKV", [P, QKV])
        WR = sb("WR", [P, HD])
        WO = sb("WO", [P, PAIRS, D])
        WF1 = sb("WF1", [P, DF])
        WF2 = sb("WF2", [P, FT, D])
        BF1 = sb("BF1", [P, FT])
        LN = sb("LN", [P, LNP, D])
        U = sb("U", [P, PAIRS])
        V_ = sb("V_", [P, PAIRS])
        RT = sb("RT", [P, S])
        ident = sb("ident", [P, P])
        Q1 = sb("Q1", [P, 2, 2, S], F32R)
        K1 = sb("K1", [P, 2, 2, S], F32R)
        K2 = sb("K2", [P, 2, 2, S], F32R)
        KR = sb("KR", [P, PAIRS, S])
        KS = sb("KS", [P, S])
        BD = sb("BD", [P, PAIRS * HEADS])
        CR = sb("CR", [P, CS, S])
        VV = sb("VV", [P, 2, KT, P])
        PR = sb("PR", [P, 4, S])
        PT = sb("PT", [P, 2, 2, KT, S])
        VEC = sb("VEC", [P, PAIRS, S])
        F = sb("F", [P, FT, S])
        Y = sb("Y", [P, KT, D])
        Z = sb("Z", [P, KT, D])
        YT = sb("YT", [P, S])
        ST = sb("ST", [P, NT, 6])
        MV = sb("MV", [P, NT, 2])
        VE = sb("VE", [P, NT])
        RS = sb("RS", [P, NT])
        HALF = sb("HALF", [P, NT])
        MIN = sb("MIN", [P, 8])
        SUM = sb("SUM", [P, 8])
        RC = sb("RC", [P, 8])
        EWO = VEC[:, :, :].rearrange("p a b -> p (a b)").rearrange("p (e f d) -> p e f d", e=E, f=FT)
        HID = PT[:, 0].rearrange("p a b c -> p (a b c)").rearrange("p (s f n) -> p s f n", s=2, f=FT)
        EWI = KR[:, :, :].rearrange("p a b -> p (a b)").rearrange("p (e f) -> p e f", e=E)
        late = PT[:, 1].rearrange("p a b c -> p (a b c)")
        GWI = late[:, 0:DF]
        GWO = late[:, DF:DF + FT * D].rearrange("p (f d) -> p f d", f=FT)
        at = DF + FT * D
        EBO = late[:, at:at + E * D].rearrange("p (e d) -> p e d", e=E)
        at += E * D
        GBO = late[:, at:at + D]
        GBI = late[:, at + D:at + D + FT]
        at += D + FT
        EBI = late[:, at:at + E * FT].rearrange("p (e f) -> p e f", e=E)
        EX = PR
        RL = F
        ACC = Z
        TOP = sb("TOP", [P, KT, 8])
        TIX = sb("TIX", [P, KT, 8], U32)
        TIF = sb("TIF", [P, KT, 8])
        W12 = sb("W12", [P, KT, 2, E])
        WS = sb("WS", [P, KT, 2])
        WG = sb("WG", [P, KT, E])
        IOTA = sb("IOTA", [P, E])

        SB = [ps(f"SB{i}") for i in range(3)]
        TB = [ps(f"TB{i}") for i in range(2)]
        PVB = ps("PVB")
        PJ = [ps(f"PJ{i}") for i in range(2)]
        FB = [SB[0], SB[1], SB[2], PVB]

        ld_x, ld_c, ld_k, ld_moe, ld_ewo = (sem(n) for n in ("ld_x", "ld_c", "ld_k", "ld_moe", "ld_ewo"))
        ld_q, ld_r = sem("ld_q"), sem("ld_r")
        ld_o = sem("ld_o")
        ident_ok = sem("ident_ok")
        dve_ok = sem("dve_ok")
        var_ok, rstd_ok = sem("var_ok"), sem("rstd_ok")
        exp_c, cb_ok, mod_ok, mod_in = sem("exp_c"), sem("cb_ok"), sem("mod_ok"), sem("mod_in")
        norm_ok, tr_ok, tr_in = sem("norm_ok"), sem("tr_ok"), sem("tr_in")
        uv_ok, htc_ok, wq_ok = sem("uv_ok"), sem("htc_ok"), sem("wq_ok")
        qh_ok, kh_ok, k_ok = sem("qh_ok"), sem("kh_ok"), sem("k_ok")
        c_out = sem("c_out")
        c_in = [sem(f"c{i}_in") for i in range(CS)]
        terms_d = nc.dram_tensor("key_terms", [L, HEADS, S], F32).ap()
        fill_ok = sem("fill_ok")
        bank_in = [sem(f"bank{i}_in") for i in range(2)]
        score_ok, min_ok, exp_ok, rec_ok, prob_ok = (sem(n) for n in ("score_ok", "min_ok", "exp_ok", "rec_ok", "prob_ok"))
        pt_ok, pv_ok, vec_in = sem("pt_ok"), sem("pv_ok"), sem("vec_in")
        pt_in = [sem(f"pt{i}_in") for i in range(2)]
        h1_ok, h2_ok = sem("h1_ok"), sem("h2_ok")
        e1_ok, ee_ok, er_ok, et_ok, eh_ok, e2_ok, ey_ok, fin_ok, st_out = (
            sem(n) for n in ("e1_ok", "ee_ok", "er_ok", "et_ok", "eh_ok", "e2_ok", "ey_ok", "fin_ok", "st_out"))

        def fills_before(l, b):
            return l * LAYER_FILLS + b * len(BODY) + len(PROLOGUE)

        def on_bank_before(k, l, b):
            return l * LAYER_ON[k] + b * BODY_ON[k] + (PRO_ON[k] + 1)

        def item_before(it):
            return ((it + (B - 1)) & (B - 1)) + (it < 1)

        def pt_on_act(t):
            return t % 4 == 1

        def pt_of(t):
            p, r = divmod(t, TPP)
            h, q = divmod(r, KT)
            return PT[:, p % 2, h, :, q * P:(q + 1) * P]

        block = ctx.enter_context(nc.Block())

        @block.sync
        def _(sp):
            xt = x_d.rearrange("b (t p) d -> p (b t) d", p=P)
            ot = out_d.rearrange("b (t p) d -> p b t d", p=P)
            sp.dma_start(X[:, :].rearrange("p (t d) -> p t d", d=D), xt).then_inc(ld_x, 16)
            sp.dma_start(CT[:, :], c_d).then_inc(ld_c, 16)
            sp.dma_start(WM[:, :], wmod_d).then_inc(ld_c, 16)

            def load_r(l):
                sp.dma_start(WR[:, :], wr_d[l]).then_inc(ld_r, 16)

            def load_q(l, fills=None):
                src = wqkv_d[l].rearrange("d (t n) -> d t n", t=3)
                dst = WQKV[:, :].rearrange("p (t n) -> p t n", t=3)
                if fills is not None:
                    wait_alone(sp, fill_ok, fills + BODY["v", LAST][0])
                sp.dma_start(dst[:, :, P:HD], src[:, :, P:HD]).then_inc(ld_q, 16)
                if fills is not None:
                    wait_alone(sp, fill_ok, fills + BODY["v", PAIRS][0])
                sp.dma_start(dst[:, :, 0:P], src[:, :, 0:P]).then_inc(ld_q, 16)

            def load_o(l):
                sp.dma_start(WO[:, :, :], wo_d[l].rearrange("(a p) d -> p a d", p=P)).then_inc(ld_o, 16)
                sp.dma_start(WF1[:, :], wf1_d[l]).then_inc(ld_o, 16)
                sp.dma_start(WF2[:, :, :], wf2_d[l].rearrange("(a p) d -> p a d", p=P)).then_inc(ld_o, 16)
                sp.dma_start(BF1[:, :], bf1_d[l]).then_inc(ld_o, 16)
                for n, row in enumerate((ln1g_d, ln1b_d, ln2g_d, ln2b_d)):
                    sp.dma_start(LN[:, n, :], row[l].partition_broadcast(P)).then_inc(ld_o, 16)
                sp.dma_start(LN[:, 4, :], bf2_d[l].partition_broadcast(P)).then_inc(ld_o, 16)

            load_r(0)
            sp.dma_start(RT[:, :], rt_d).then_inc(ld_o, 16)
            sp.dma_start(U[:, :], u_d).then_inc(ld_k, 16)
            sp.dma_start(V_[:, :], v_d).then_inc(ld_k, 16)
            load_q(0)
            load_o(0)

            def load_terms(l, it):
                tiles = sp.snap(it * STEPS)
                for h in range(HEADS):
                    wait_alone(sp, min_ok, tiles + (h + 1) * KT)
                    sp.dma_start(CR[:, h % CS, :], terms_d[l, h].partition_broadcast(P)).then_inc(c_in[h % CS], 16)

            with sp.Fori(0, L) as l:
                _, k, n = PROLOGUE["c", 0]
                wait_alone(sp, bank_in[k], l * LAYER_ON[k] + (n + 1))
                sp.dma_start(terms_d[l], Y[0:HEADS, :, :].rearrange("p a b -> p (a b)")).then_inc(c_out, 16)
                wait_alone(sp, c_out, (l + 1) * 16)
                load_terms(l, l * B)
                _, k, n = BODY["h2", 0]
                wait_alone(sp, bank_in[k], on_bank_before(k, l, 0) + n)
                load_o(l)
                load_r((l + 1) & (L - 1))
                with sp.Fori(1, B) as b:
                    load_terms(l, l * B + b)
                load_q((l + 1) & (L - 1), fills_before(l, B - 1))
            sp.wait_ge(fill_ok, L * LAYER_FILLS + END["o", 0][0])
            for dst, src in ((GWI, gwi_d), (GWO, gwo_d.rearrange("(a p) d -> p a d", p=P)), (GBI, gbi_d),
                             (EBI, ebi_d), (GBO, gbo_d.partition_broadcast(P)),
                             (EBO, ebo_d.rearrange("e d -> (e d)").partition_broadcast(P).rearrange("p (e d) -> p e d", e=E))):
                sp.dma_start(dst, src).then_inc(ld_moe, 16)
            sp.dma_start(EWI, ewi_d.rearrange("e p f -> p e f")).then_inc(ld_ewo, 16)
            for e in range(E):
                sp.dma_start(EWO[:, e], ewo_d[e].rearrange("(a p) d -> p a d", p=P)).then_inc(ld_ewo, 16)
            for g in range(B):
                sp.wait_ge(fin_ok, g + 1)
                sp.dma_start(ot[:, g], X[:, g * S:(g + 1) * S].rearrange("p (t d) -> p t d", d=D)).then_inc(st_out, 16)
            sp.wait_ge(st_out, 16 * B)

        @block.gpsimd
        def _(pool):
            nc.gpsimd.memset(ident[:, :], 0.0).then_inc(ident_ok, 1)
            pool.wait_ge(ident_ok, 1)
            nc.gpsimd.affine_select(out=ident[:, :], in_=ident[:, :], compare_op=ALU.not_equal, fill=1.0, base=0,
                                    pattern=[[-1, P]], channel_multiplier=1).then_inc(ident_ok, 1)
            nc.gpsimd.iota(IOTA[:, :], [[1, E]], base=0, channel_multiplier=0,
                           allow_small_or_imprecise_dtypes=True).then_inc(ident_ok, 1)
            nc.gpsimd.memset(HALF[:, :], -0.5).then_inc(ident_ok, 1)
            pool.wait_ge(ident_ok, 4)

            def rstd(n, tiles):
                pool.wait_ge(var_ok, n)
                nc.gpsimd.tensor_tensor(RS[:, 0:tiles], VE[:, 0:tiles], HALF[:, 0:tiles], ALU.pow).then_inc(rstd_ok, 1)

            rstd(1, NT)
            with pool.Fori(0, L) as l:
                wait_alone(pool, ld_q, (l + 1) * (16 * LOADS_Q))
                nc.gpsimd.tensor_scalar(WQKV[:, 0:HD], WQKV[:, 0:HD], -QS, 1.0, ALU.mult, ALU.mult).then_inc(wq_ok, 1)
                with pool.Fori(0, B) as b:
                    it = pool.snap(l * B + b)
                    tiles = pool.snap(it * STEPS)
                    for t in range(STEPS):
                        wait_alone(pool, rec_ok, tiles + (t + 1))
                        pr = PR[:, t % 4, :]
                        nc.gpsimd.tensor_scalar(pr, pr, RC[:, t % 8:t % 8 + 1], 1.0, ALU.mult, ALU.mult
                                                ).then_inc(prob_ok, 1)
                        if t == Y_AT + 1:
                            rstd(it * 2 + 2, KT)
                        if t == Z_AT + 1:
                            rstd(it * 2 + 3, KT)
            rstd(2 * L * B + 2, KT)
            rstd(2 * L * B + 3, KT)
            rstd(2 * L * B + 4, NT)
            with pool.Fori(0, B) as g:
                tiles = pool.snap(g * (UNITS * FT))
                for j in range(UNITS * FT):
                    wait_alone(pool, ee_ok, tiles + (j + 1))
                    e = EX[:, j % 4, :]
                    nc.gpsimd.tensor_scalar(e, e, 1.0, -1.0, ALU.min, ALU.add).then_inc(et_ok, 1)

        @block.scalar
        def _(act):
            act.wait_ge(ld_c, 32)
            nc.scalar.activation(CE[:, :], CT[:, :], ACT.Exp, scale=-1.0).then_inc(exp_c, 1)
            act.wait_ge(uv_ok, 1)

            def high_q(p, bank):
                c = p % PAIRS
                for h in range(2):
                    r = slice(h * DH, (h + 1) * DH)
                    last = nc.scalar.activation(Q1[r, p % 2, h, :], bank[r, :], ACT.Identity, bias=U[r, c:c + 1])
                return last

            def high_k(p, h, table, on_bank):
                r = slice(h * DH, (h + 1) * DH)
                if h == 0:
                    _, k, m = table["k", p]
                    act.wait_ge(bank_in[k], on_bank[k] + m)
                nc.scalar.copy(K1[0:DH, p % 2, h, :], KS[r, :])
                last = nc.scalar.copy(K1[DH:P, p % 2, h, :], KS[r, :])
                if h == 1:
                    last.then_inc(kh_ok, 1)

            def take_v(p, bank):
                return nc.scalar.copy(VV[:, p % 2], bank[:, :].rearrange("p (t d) -> p t d", d=P))

            def take_fill(key, table, fills, slot):
                kind, p = key
                n, k, _ = table[key]
                bank = PJ[k]
                act.wait_ge(fill_ok, fills + n)
                if kind == "q":
                    high_q(p, bank).then_inc(qh_ok, 1)
                elif kind == "kr":
                    nc.scalar.copy(KR[:, p, :], bank[:, :]).then_inc(bank_in[k], 1)
                elif kind == "c":
                    nc.scalar.copy(Y[0:HEADS, :, :].rearrange("p a b -> p (a b)"), bank[0:HEADS, :]).then_inc(bank_in[k], 1)
                elif kind == "v":
                    take_v(p, bank).then_inc(bank_in[k], 1)
                elif kind == "h1":
                    nc.scalar.copy(YT[:, :], bank[:, :]).then_inc(bank_in[k], 1)
                elif kind == "f1":
                    nc.scalar.activation(F[:, p, :], bank[:, :], ACT.Relu, bias=BF1[:, p:p + 1]).then_inc(bank_in[k], 1)
                elif kind == "h2":
                    nc.scalar.copy(HT[:, bass.ts(slot, S)], bank[:, :]).then_inc(bank_in[k], 1)

            def on_act(key):
                return key[0] in ("q", "c", "v", "h1", "h2") or key[0] in ("f1", "kr") and key[1] % 2 == 0

            with act.Fori(0, L) as l:
                start = act.snap(l * LAYER_FILLS)
                for key in PROLOGUE:
                    if on_act(key):
                        take_fill(key, PROLOGUE, start, 0)
                    if key == ("k", 0):
                        for h in range(2):
                            high_k(0, h, PROLOGUE, [l * LAYER_ON[k] + 1 for k in range(2)])
                with act.Fori(0, B) as b:
                    it = act.snap(l * B + b)
                    slot = act.snap(item_before(it))
                    tiles = act.snap(it * STEPS)
                    fills = act.snap(fills_before(l, b))
                    on_bank = [act.snap(on_bank_before(k, l, b)) for k in range(2)]

                    def take_vec(p):
                        act.wait_ge(pv_ok, it * PAIRS + (p + 1))
                        nc.scalar.copy(VEC[:, p, :], PVB[:, :]).then_inc(vec_in, 1)

                    for t in range(STEPS):
                        act.wait_ge(min_ok, tiles + (t + 1 + CS * KT))
                        if t >= 4:
                            act.wait_ge(pt_ok, tiles + (t - 3))
                        nc.scalar.activation(PR[:, t % 4, :], SB[t % 3][:, :], ACT.Exp, bias=MIN[:, t % 8:t % 8 + 1],
                                             scale=-1.0, accum_out=SUM[:, t % 8:t % 8 + 1]).then_inc(exp_ok, 1)
                        if t >= 2 and pt_on_act(t - 2):
                            act.wait_ge(pt_ok, tiles + (t - 1))
                            nc.scalar.copy(pt_of(t - 2), TB[t % 2][:, :].rearrange("p (t d) -> p t d", d=P)
                                           ).then_inc(pt_in[t % 2], 1)
                        if t in at_step and on_act(at_step[t]):
                            take_fill(at_step[t], BODY, fills, slot)
                        p, r = divmod(t, TPP)
                        if r in (4, 5):
                            high_k(p + 1, r - 4, BODY, on_bank)
                        if r == 6 and 1 <= p < LAST:
                            take_vec(p - 1)
                    take_vec(LAST - 1)
                    take_fill(("v", PAIRS), BODY, fills, slot)
                    take_vec(LAST)
            for key in END:
                if on_act(key):
                    take_fill(key, END, L * LAYER_FILLS, B - 1)
            act.wait_ge(ld_moe, 16 * 6)
            with act.Fori(0, B) as g:
                tiles = act.snap(g * (UNITS * FT))
                for j in range(UNITS * FT):
                    u, f = divmod(j, FT)
                    bias = GBI[:, f:f + 1] if u == 0 else EBI[:, u - 1, f:f + 1]
                    act.wait_ge(e1_ok, tiles + (j + 1))
                    if j >= 4:
                        act.wait_ge(eh_ok, tiles + (j - 3))
                    nc.scalar.activation(EX[:, j % 4, :], FB[j % 4][:, :], ACT.Exp, bias=bias).then_inc(ee_ok, 1)

        @block.vector
        def _(dve):
            v = nc.vector

            def norm_stats(src, tiles, link, n):
                for t in range(tiles):
                    last = v.bn_stats(ST[:, t, :], src[:, t * D:(t + 1) * D])
                link(last)
                for t in range(tiles):
                    last = v.bn_aggr(MV[:, t, :], ST[:, t, :])
                link(last)
                v.tensor_scalar(VE[:, 0:tiles], MV[:, 0:tiles, 1], EPS, None, ALU.add).then_inc(var_ok, 1)
                wait_alone(dve, rstd_ok, n)

            def normalise(dst, src, tiles, link):
                for t in range(tiles):
                    last = v.tensor_scalar(dst[:, t * D:(t + 1) * D], src[:, t * D:(t + 1) * D], MV[:, t, 0:1],
                                           RS[:, t:t + 1], ALU.subtract, ALU.mult)
                link(last)

            def row(ap):
                return ap.unsqueeze(1).to_broadcast([P, KT, D])

            def tk(ap):
                return ap.rearrange("p (t d) -> p t d", d=D)

            def chain(base):
                n = [0]

                def link(ins):
                    n[0] += 1
                    ins.then_inc(dve_ok, 1)
                    if isinstance(base, int):
                        dve.wait_ge(dve_ok, base + n[0])
                    else:
                        wait_alone(dve, dve_ok, base + n[0])
                return link, n

            link, n0 = chain(0)
            dve.wait_ge(exp_c, 1)
            link(v.tensor_scalar(CE[:, :], CE[:, :], 1.0, None, ALU.add))
            link(v.reciprocal(CE[:, :], CE[:, :]))
            link(v.tensor_tensor(CE[:, :], CE[:, :], CT[:, :], ALU.mult))
            v.tensor_copy(CB[:, :, :], CE[:, :].unsqueeze(2).to_broadcast([P, B, P])).then_inc(cb_ok, 1)

            dve.wait_ge(ld_k, 32)
            link(v.tensor_scalar(U[:, :], U[:, :], -QS, None, ALU.mult))
            link(v.scalar_tensor_tensor(out=V_[:, :], in0=V_[:, :], scalar=-QS, in1=U[:, :], op0=ALU.mult,
                                        op1=ALU.subtract))
            link(v.memset(BD[:, :], 0.0))
            for h in range(2):
                r = slice(h * DH, (h + 1) * DH)
                v.tensor_copy(BD[r, h:PAIRS * HEADS:HEADS + 2], V_[r, :])
                v.memset(K2[DH - h * DH:P - h * DH, :, h, :].bitcast(F32), 0.0)
            v.tensor_copy(VE[:, 0:1], U[:, 0:1]).then_inc(uv_ok, 1)

            def take_mod(n):
                for b in range(B):
                    dve.wait_ge(mod_ok, n * B + b + 1)
                    last = v.tensor_copy(MOD[:, b, :], PJ[b % 2][:, 0:3 * D])
                    last.then_inc(mod_in, 1)
                dve.wait_ge(mod_in, (n + 1) * B)

            def modulated(n, link):
                norm_stats(X, NT, link, n)
                normalise(H, X, NT, link)
                for b in range(B):
                    h = tk(H[:, b * S:(b + 1) * S])
                    last = v.scalar_tensor_tensor(out=h, in0=row(MOD[:, b, D:2 * D]), scalar=1.0, in1=h,
                                                  op0=ALU.add, op1=ALU.mult)
                link(last)
                for b in range(B):
                    h = tk(H[:, b * S:(b + 1) * S])
                    v.tensor_tensor(h, h, row(MOD[:, b, 0:D]), ALU.add).then_inc(norm_ok, 1)

            def take_transposed(n):
                for b in range(B):
                    dve.wait_ge(tr_ok, n * B + b + 1)
                    v.tensor_copy(HT[:, b * S:(b + 1) * S], TB[b % 2][:, :]).then_inc(tr_in, 1)

            def signed_gate(link):
                g = MOD[:, :, 2 * D:3 * D]
                a, s = tk(Y[:, :, :].rearrange("p a b -> p (a b)")), tk(Z[:, :, :].rearrange("p a b -> p (a b)"))
                link(v.scalar_tensor_tensor(out=a, in0=g, scalar=-1.0, in1=g, op0=ALU.mult, op1=ALU.max))
                link(v.tensor_scalar(a, a, 0.25, None, ALU.max))
                link(v.tensor_scalar(s, g, 0.0, 2.0, ALU.is_ge, ALU.mult))
                link(v.scalar_tensor_tensor(out=g, in0=s, scalar=-1.0, in1=a, op0=ALU.add, op1=ALU.mult))

            take_mod(0)
            dve.wait_ge(ld_x, 16)
            modulated(1, link)
            take_transposed(0)
            dve.wait_ge(tr_in, B)
            v.tensor_copy(HTC[:, :], HT[:, 0:S])
            v.memset(H[:, B * S:(B + 1) * S], 0.0)
            v.memset(VEC[:, :, :].rearrange("p a b -> p (a b)"), 0.0).then_inc(htc_ok, 1)
            dve.wait_ge(htc_ok, 1)
            dve.sem_inc(bank_in[0], 1)
            dve.sem_inc(bank_in[1], 1)
            dve.sem_inc(vec_in, 1)
            dve.sem_inc(min_ok, CS * KT)
            signed_gate(link)
            before = n0[0]

            LINKS = 9
            y, z = Y[:, :, :].rearrange("p a b -> p (a b)"), Z[:, :, :].rearrange("p a b -> p (a b)")

            def finish(n, it, slot, link, table, fills):
                def bank_of(key):
                    m, k, _ = table[key]
                    dve.wait_ge(fill_ok, fills + m)
                    return PJ[k], bank_in[k]

                if n == 0:
                    bank, free = bank_of(("o", 0))
                    v.tensor_tensor(y, bank[:, :], H[:, bass.ts(slot, S)], ALU.add).then_inc(free, 1)
                    wait_alone(dve, free, bank_total(table, ("o", 0)))
                elif n in (1, 7):
                    for t in range(KT):
                        last = v.bn_stats(ST[:, t, :], (y, z)[n == 7][:, t * D:(t + 1) * D])
                    link(last)
                elif n in (2, 8):
                    for t in range(KT):
                        last = v.bn_aggr(MV[:, t, :], ST[:, t, :])
                    link(last)
                    v.tensor_scalar(VE[:, 0:KT], MV[:, 0:KT, 1], EPS, None, ALU.add).then_inc(var_ok, 1)
                elif n in (3, 9):
                    wait_alone(dve, rstd_ok, it * 2 + (2 if n == 3 else 3))
                    normalise(*((y, y) if n == 3 else (z, z)), KT, link)
                elif n == 4:
                    link(v.tensor_tensor(tk(y), tk(y), row(LN[:, 0, :]), ALU.mult))
                elif n == 5:
                    v.tensor_tensor(tk(y), tk(y), row(LN[:, 1, :]), ALU.add).then_inc(h1_ok, 1)
                elif n == 6:
                    bank, free = bank_of(("f2", 0))
                    v.tensor_tensor(tk(z), tk(bank[:, :]), row(LN[:, 4, :]), ALU.add).then_inc(free, 1)
                    wait_alone(dve, free, bank_total(table, ("f2", 0)))
                elif n == 10:
                    link(v.tensor_tensor(tk(z), tk(z), row(LN[:, 2, :]), ALU.mult))
                elif n == 11:
                    v.tensor_tensor(tk(z), tk(z), row(LN[:, 3, :]), ALU.add).then_inc(h2_ok, 1)
                elif n == 12:
                    wait_alone(dve, h2_ok, it + 1)
                    link(v.tensor_copy(H[:, bass.ts(slot, S)], z))

            def low_q(p, table, pairs):
                _, k, _ = table["q", p]
                c = p % PAIRS
                dve.wait_ge(qh_ok, pairs + (p + 1))
                for h in range(2):
                    r, o = slice(h * DH, (h + 1) * DH), slice(DH - h * DH, P - h * DH)
                    last = v.scalar_tensor_tensor(out=Q1[o, p % 2, h, :], in0=PJ[k][r, :], scalar=U[r, c:c + 1],
                                                  in1=Q1[r, p % 2, h, :].bitcast(F32), op0=ALU.add, op1=ALU.subtract)
                last.then_inc(bank_in[k], 1)

            def sum_k(p, table, fills):
                n, k, m = table["k", p]
                dve.wait_ge(fill_ok, fills + n)
                v.tensor_tensor(KS[:, :], PJ[k][:, :], KR[:, p % PAIRS, :], ALU.add).then_inc(bank_in[k], 1)

            def low_k(p, pairs):
                dve.wait_ge(kh_ok, pairs + (p + 1))
                for h in range(2):
                    r = slice(h * DH, (h + 1) * DH)
                    last = v.tensor_tensor(K2[r, p % 2, h, :], KS[r, :], K1[r, p % 2, h, :].bitcast(F32), ALU.subtract)
                last.then_inc(k_ok, 1)

            def take_relu(f, table, fills):
                m, k, _ = table["f1", f]
                dve.wait_ge(fill_ok, fills + m)
                v.tensor_scalar(F[:, f, :], PJ[k][:, :], BF1[:, f:f + 1], 0.0, ALU.add, ALU.max).then_inc(bank_in[k], 1)

            with dve.Fori(0, L) as l:
                start, pairs = dve.snap(l * LAYER_FILLS), dve.snap(l * LAYER_PAIRS)
                for p in range(1, PAIRS, 2):
                    n, k, _ = PROLOGUE["kr", p]
                    dve.wait_ge(fill_ok, start + n)
                    v.tensor_copy(KR[:, p, :], PJ[k][:, :]).then_inc(bank_in[k], 1)
                low_q(0, PROLOGUE, pairs)
                sum_k(0, PROLOGUE, start)
                low_k(0, pairs)
                with dve.Fori(0, B) as b:
                    it = dve.snap(l * B + b)
                    slot = dve.snap(item_before(it))
                    tiles = dve.snap(it * STEPS)
                    fills = dve.snap(fills_before(l, b))
                    pairs = dve.snap(l * LAYER_PAIRS + b * PAIRS)
                    links = dve.snap(it * LINKS + before)
                    link, n1 = chain(links)

                    def bank_total(table, key):
                        return on_bank_before(table[key][1], l, b) + table[key][2]

                    def reciprocal(t):
                        dve.wait_ge(exp_ok, tiles + (t + 1))
                        v.reciprocal(RC[:, t % 8:t % 8 + 1], SUM[:, t % 8:t % 8 + 1]).then_inc(rec_ok, 1)

                    def take_pt(t):
                        p, r = divmod(t, TPP)
                        dve.wait_ge(pt_ok, tiles + (t + 1))
                        if p >= 2 and r == 0:
                            dve.wait_ge(pv_ok, it * PAIRS + (p - 1))
                        v.tensor_copy(pt_of(t), TB[t % 2][:, :].rearrange("p (t d) -> p t d", d=P)
                                      ).then_inc(pt_in[t % 2], 1)

                    for t in range(STEPS):
                        if t >= 1:
                            reciprocal(t - 1)
                        p, r = divmod(t, TPP)
                        h = t // KT
                        if t % KT == 0:
                            wait_alone(dve, c_in[h % CS], it * (HEADS // CS * 16) + (h // CS + 1) * 16)
                        wait_alone(dve, score_ok, tiles + (t + 1))
                        s = SB[t % 3][:, :]
                        v.tensor_tensor_reduce(out=s, in0=s, in1=CR[:, h % CS, :], scale=1.0, scalar=3e38, op0=ALU.add,
                                               op1=ALU.min, accum_out=MIN[:, t % 8:t % 8 + 1]).then_inc(min_ok, 1)
                        if t >= 2 and not pt_on_act(t - 2):
                            take_pt(t - 2)
                        if r == 2:
                            low_q(p + 1, BODY, pairs)
                        if r == 3:
                            sum_k(p + 1, BODY, fills)
                        if r == 6:
                            low_k(p + 1, pairs)
                        if Y_AT <= t < Y_AT + 6:
                            finish(t - Y_AT, it, slot, link, BODY, fills)
                        if Z_AT <= t < Z_AT + 7:
                            finish(6 + t - Z_AT, it, slot, link, BODY, fills)
                        if t in at_step and at_step[t][0] == "f1" and at_step[t][1] % 2:
                            take_relu(at_step[t][1], BODY, fills)
                        if t == HTC_AT:
                            dve.wait_ge(fill_ok, fills + BODY["v", LAST][0])
                            _, k, _ = BODY["h2", 0]
                            wait_alone(dve, bank_in[k], bank_total(BODY, ("h2", 0)))
                            v.tensor_copy(HTC[:, :], HT[:, bass.ts((b + 1) & (B - 1), S)]).then_inc(htc_ok, 1)
                    reciprocal(STEPS - 1)
                    assert not pt_on_act(STEPS - 2) and not pt_on_act(STEPS - 1)
                    take_pt(STEPS - 2)
                    take_pt(STEPS - 1)
                    assert n1[0] == LINKS, n1
            link, n1 = chain(L * B * LINKS + before)

            def bank_total(table, key):
                return L * LAYER_ON[table[key][1]] + table[key][2] + 1

            for n in range(6):
                finish(n, L * B, B - 1, link, END, L * LAYER_FILLS)
            for f in range(1, FT, 2):
                take_relu(f, END, L * LAYER_FILLS)
            for n in range(6, 13):
                finish(n, L * B, B - 1, link, END, L * LAYER_FILLS)

            link, n2 = chain((L * B + 1) * LINKS + before)

            def add_branch(x, branch, b):
                link(v.tensor_tensor(branch, branch, row(MOD[:, b, 2 * D:3 * D]), ALU.mult))
                return v.tensor_tensor(x, x, branch, ALU.add)

            dve.wait_ge(dve_ok, (L * B + 1) * LINKS + before)
            for b in range(B):
                last = add_branch(tk(X[:, b * S:(b + 1) * S]), tk(H[:, b * S:(b + 1) * S]), b)
            link(last)
            take_mod(1)
            modulated(2 * L * B + 4, link)
            take_transposed(1)
            dve.wait_ge(tr_in, 2 * B)
            signed_gate(link)
            before2 = (L * B + 1) * LINKS + before + n2[0]

            dve.wait_ge(ld_moe, 16 * 6)
            dve.wait_ge(ident_ok, 4)
            TILES = UNITS * FT
            y, acc = Y[:, :, :], ACC[:, :, :]
            GLINKS = 8 + UNITS - 1
            with dve.Fori(0, B) as g:
                tiles = dve.snap(g * TILES)
                links = dve.snap(g * GLINKS + before2)
                link, n3 = chain(links)

                def positive(j):
                    u, f = divmod(j, FT)
                    bias = GBI[:, f:f + 1] if u == 0 else EBI[:, u - 1, f:f + 1]
                    dve.wait_ge(ee_ok, tiles + (j + 1))
                    v.tensor_scalar(RL[:, j % 4, :], FB[j % 4][:, :], bias, 0.0, ALU.add, ALU.max).then_inc(er_ok, 1)

                def selu(j):
                    u, f = divmod(j, FT)
                    if u >= 2 and f == 0:
                        dve.wait_ge(e2_ok, g * UNITS + (u - 1))
                    dve.wait_ge(et_ok, tiles + (j + 1))
                    dve.wait_ge(er_ok, tiles + (j + 1))
                    v.scalar_tensor_tensor(out=HID[:, u % 2, f, :], in0=EX[:, j % 4, :], scalar=SELU_ALPHA,
                                           in1=RL[:, j % 4, :], op0=ALU.mult, op1=ALU.add).then_inc(eh_ok, 1)

                def top2():
                    for t in range(KT):
                        last = v.max(TOP[:, t, :], Y[:, t, :])
                    link(last)
                    for t in range(KT):
                        last = v.max_index(TIX[:, t, :], TOP[:, t, :], Y[:, t, :])
                    link(last)
                    v.tensor_copy(TIF[:, :, :], TIX[:, :, :])
                    link(v.tensor_tensor(WS[:, :, 0:1], TOP[:, :, 0:1], TOP[:, :, 1:2], ALU.add))
                    link(v.reciprocal(WS[:, :, 1:2], WS[:, :, 0:1]))
                    link(v.tensor_tensor(TOP[:, :, 0:2], TOP[:, :, 0:2], WS[:, :, 1:2].to_broadcast([P, KT, 2]), ALU.mult))
                    for t in range(KT):
                        for k in range(2):
                            last = v.tensor_scalar(W12[:, t, k, :], IOTA[:, :], TIF[:, t, k:k + 1], TOP[:, t, k:k + 1],
                                                   ALU.is_equal, ALU.mult)
                    link(last)
                    link(v.tensor_tensor(WG[:, :, :], W12[:, :, 0, :], W12[:, :, 1, :], ALU.add))

                def take_out(u):
                    dve.wait_ge(e2_ok, g * UNITS + (u + 1))
                    bias = GBO[:, :] if u == 0 else EBO[:, u - 1, :]
                    ins = v.scalar_tensor_tensor(out=y, in0=tk(PJ[u % 2][:, :]), scalar=SELU_SCALE, in1=row(bias),
                                                 op0=ALU.mult, op1=ALU.add)
                    ins.then_inc(ey_ok, 1)
                    wait_alone(dve, ey_ok, g * UNITS + (u + 1))
                    if u == 0:
                        top2()
                        return
                    for t in range(KT):
                        w = WG[:, t, u - 1:u]
                        if u == 1:
                            last = v.tensor_scalar(ACC[:, t, :], Y[:, t, :], w, None, ALU.mult)
                        else:
                            last = v.scalar_tensor_tensor(out=ACC[:, t, :], in0=Y[:, t, :], scalar=w,
                                                          in1=ACC[:, t, :], op0=ALU.mult, op1=ALU.add)
                    link(last)

                for j in range(TILES):
                    positive(j)
                    if j >= 1:
                        selu(j - 1)
                    if j % FT == FT - 1 and j >= 2 * FT - 1:
                        take_out(j // FT - 1)
                selu(TILES - 1)
                take_out(UNITS - 1)
                gate = MOD[:, :, :].rearrange("p b d -> p (b d)")[:, bass.ts(g * 3 + 2, D)]
                link(v.tensor_tensor(acc, acc, gate.unsqueeze(1).to_broadcast([P, KT, D]), ALU.mult))
                x = X[:, bass.ts(g, S)]
                v.tensor_tensor(x, x, ACC[:, :, :].rearrange("p a b -> p (a b)"), ALU.add).then_inc(fin_ok, 1)
                assert n3[0] == GLINKS, n3

        @block.tensor
        def _(pe):
            mm = nc.tensor.matmul

            def mod_rows(n):
                for b in range(B):
                    i = n * B + b
                    if i >= 2:
                        pe.wait_ge(mod_in, i - 1)
                    mm(PJ[b % 2][:, 0:3 * D], CB[:, b, :], WM[:, n * 3 * D:(n + 1) * 3 * D], start=True, stop=True
                       ).then_inc(mod_ok, 1)

            def transposes(bank, src, done):
                for t in range(KT):
                    last = nc.tensor.transpose(bank[:, t * P:(t + 1) * P], src[:, t * P:(t + 1) * P], ident[:, :])
                last.then_inc(done, 1)

            def transpose_all(n):
                for b in range(B):
                    pe.wait_ge(norm_ok, n * B + b + 1)
                    if b >= 2:
                        pe.wait_ge(tr_in, n * B + b - 1)
                    transposes(TB[b % 2], H[:, b * S:(b + 1) * S], tr_ok)

            pe.wait_ge(cb_ok, 1)
            pe.wait_ge(ld_c, 32)
            mod_rows(0)
            pe.wait_ge(ident_ok, 4)
            transpose_all(0)
            pe.wait_ge(htc_ok, 1)
            pe.wait_ge(ld_o, 16)
            pe.wait_ge(uv_ok, 1)

            def part(key, table, fills, on_bank, params, done_pairs, first=True, last=True):
                kind, p = key
                n, k, m = table[key]
                bank = PJ[k]
                if first:
                    pe.wait_ge(bank_in[k], on_bank[k] + (m - 1))
                if table is PROLOGUE and key == ("q", 0):
                    pe.wait_ge(ld_q, params)
                    pe.wait_ge(wq_ok, done_pairs)
                if table is PROLOGUE and key == ("kr", 0):
                    pe.wait_ge(ld_r, params)
                if kind in ("q", "k"):
                    c = (0 if kind == "q" else HD) + p % PAIRS * P
                    ins = mm(bank[:, :], WQKV[:, c:c + P], HTC[:, :], start=True, stop=True)
                elif kind == "v":
                    c = 2 * HD + p % PAIRS * P
                    for i in range(KT):
                        ins = mm(bank[:, i * P:(i + 1) * P], HTC[:, i * P:(i + 1) * P], WQKV[:, c:c + P],
                                 start=True, stop=True)
                elif kind == "kr":
                    ins = mm(bank[:, :], WR[:, p * P:(p + 1) * P], RT[:, :], start=True, stop=True)
                elif kind == "c":
                    for j in range(2):
                        if j != k:
                            pe.wait_ge(bank_in[j], on_bank[j] + table["kr", PAIRS - 1][2])
                    for i in range(PAIRS):
                        ins = mm(bank[0:HEADS, :], BD[:, i * HEADS:(i + 1) * HEADS], KR[:, i, :],
                                 start=(i == 0), stop=(i == PAIRS - 1))
                elif kind in ("o", "f2"):
                    if kind == "o" and first:
                        pe.wait_ge(ld_o, params)
                        pe.wait_ge(vec_in, done_pairs + 1)
                    if kind == "f2" and first:
                        last_on = {table["f1", f][1]: table["f1", f][2] for f in range(FT)}
                        for j, i in last_on.items():
                            if j != k:
                                pe.wait_ge(bank_in[j], on_bank[j] + i)
                    src, w, tiles_k = (VEC, WO, PAIRS) if kind == "o" else (F, WF2, FT)
                    for q in range(0 if first else KT // 2, KT if last else KT // 2):
                        for i in range(tiles_k):
                            ins = mm(bank[:, q * P:(q + 1) * P], src[:, i, q * P:(q + 1) * P], w[:, i, :],
                                     start=(i == 0), stop=(i == tiles_k - 1))
                    if not last:
                        return
                elif kind in ("h1", "h2"):
                    src = (Y if kind == "h1" else Z)[:, :, :].rearrange("p a b -> p (a b)")
                    for i in range(KT):
                        ins = nc.tensor.transpose(bank[:, i * P:(i + 1) * P], src[:, i * P:(i + 1) * P], ident[:, :])
                elif kind == "f1":
                    if p == 0:
                        _, j, i = table["h1", 0]
                        pe.wait_ge(bank_in[j], on_bank[j] + i)
                    ins = mm(bank[:, :], WF1[:, p * P:(p + 1) * P], YT[:, :], start=True, stop=True)
                ins.then_inc(fill_ok, 1)

            with pe.Fori(0, L) as l:
                fills = pe.snap(l * LAYER_FILLS)
                on_bank = [pe.snap(l * LAYER_ON[k] + 1) for k in range(2)]
                layers = pe.snap(l + 1)
                loads = {"kr": pe.snap(layers * 16), "q": pe.snap(layers * (16 * LOADS_Q))}
                for key in PROLOGUE:
                    part(key, PROLOGUE, fills, on_bank, loads.get(key[0], 0), layers)
                with pe.Fori(0, B) as b:
                    it = pe.snap(l * B + b)
                    tiles = pe.snap(it * STEPS)
                    fills = pe.snap(fills_before(l, b))
                    on_bank = [pe.snap(on_bank_before(k, l, b)) for k in range(2)]
                    pairs, k_pairs = pe.snap(it * PAIRS), pe.snap(l * LAYER_PAIRS + b * PAIRS)
                    halves = pe.snap(it * (STEPS // 2))
                    params = pe.snap((((it + (B - 1)) >> (B.bit_length() - 1)) + 1) * (16 * LOADS_O) + 16)

                    def score(t):
                        p, r = divmod(t, TPP)
                        h, q = divmod(r, KT)
                        if t == 0:
                            for k in range(2):
                                pe.wait_ge(bank_in[k], on_bank[k])
                        elif r == 0:
                            _, j, i = BODY["q", p]
                            pe.wait_ge(bank_in[j], on_bank[j] + i)
                        if r == 0:
                            pe.wait_ge(k_ok, k_pairs + (p + 1))
                        if t >= 3:
                            pe.wait_ge(exp_ok, tiles + (t - 2))
                        part_q = Q1[:, p % 2, h, q * P:(q + 1) * P]
                        mm(SB[t % 3][:, :], part_q, K1[:, p % 2, h, :], start=True, stop=False)
                        mm(SB[t % 3][:, :], part_q, K2[:, p % 2, h, :], start=False, stop=True).then_inc(score_ok, 1)

                    def turn(t):
                        pe.wait_ge(prob_ok, tiles + (t + 1))
                        if t >= 2:
                            pe.wait_ge(pt_in[t % 2], halves + t // 2)
                        transposes(TB[t % 2], PR[:, t % 4, :], pt_ok)

                    def values(p, k):
                        if k == 0:
                            if p >= 1:
                                _, j, i = BODY["v", p]
                                pe.wait_ge(bank_in[j], on_bank[j] + i)
                                pe.wait_ge(vec_in, pairs + (p + 1))
                            for i in range(2):
                                pe.wait_ge(pt_in[i], halves + (p + 1) * KT)
                        for h in range(2):
                            last = mm(PVB[h * DH:(h + 1) * DH, :], VV[:, p % 2, k, h * DH:(h + 1) * DH],
                                      PT[:, p % 2, h, k, :], start=(k == 0), stop=(k == KT - 1))
                        if k == KT - 1:
                            last.then_inc(pv_ok, 1)

                    for t in range(STEPS):
                        p, r = divmod(t, TPP)
                        score(t)
                        if t >= 2:
                            turn(t - 2)
                        if t in at_step:
                            key = at_step[t]
                            if key == ("h1", 0):
                                pe.wait_ge(h1_ok, it + 1)
                            if key == ("h2", 0):
                                pe.wait_ge(h2_ok, it + 1)
                            if key == ("q", PAIRS):
                                pe.wait_ge(htc_ok, it + 2)
                            part(key, BODY, fills, on_bank, params, pairs, last=key[0] not in ("o", "f2"))
                        elif t - 1 in at_step and at_step[t - 1][0] in ("o", "f2"):
                            part(at_step[t - 1], BODY, fills, on_bank, params, pairs, first=False)
                        if 1 <= p < LAST and 2 <= r < 2 + KT:
                            values(p - 1, r - 2)
                        if p == LAST and r >= TPP - 2:
                            values(p - 1, r - (TPP - 2))
                    values(LAST - 1, KT - 2)
                    turn(STEPS - 2)
                    values(LAST - 1, KT - 1)
                    part(("v", PAIRS), BODY, fills, on_bank, params, pairs)
                    turn(STEPS - 1)
                    for k in range(KT):
                        values(LAST, k)

            on_bank = [L * LAYER_ON[k] + 1 for k in range(2)]
            for key in END:
                if key == ("h1", 0):
                    pe.wait_ge(h1_ok, L * B + 1)
                if key == ("h2", 0):
                    pe.wait_ge(h2_ok, L * B + 1)
                part(key, END, L * LAYER_FILLS, on_bank, (L + 1) * 16 * LOADS_O + 16, L * B * PAIRS)

            for k in range(2):
                pe.wait_ge(bank_in[k], L * LAYER_ON[k] + 1 + END_ON[k])
            mod_rows(1)
            transpose_all(1)
            pe.wait_ge(tr_in, 2 * B)
            pe.wait_ge(ld_moe, 16 * 6)
            pe.wait_ge(ld_ewo, 16 * (E + 1))
            TILES = UNITS * FT
            with pe.Fori(0, B) as g:
                tiles = pe.snap(g * TILES)

                def hidden(u):
                    for f in range(FT):
                        j = u * FT + f
                        if j >= 4:
                            pe.wait_ge(er_ok, tiles + (j - 3))
                        w = GWI[:, f * P:(f + 1) * P] if u == 0 else EWI[:, u - 1, f * P:(f + 1) * P]
                        mm(FB[j % 4][:, :], w, HT[:, bass.ts(g, S)], start=True, stop=True).then_inc(e1_ok, 1)

                def second(u):
                    pe.wait_ge(eh_ok, tiles + (u + 1) * FT)
                    if u >= 2:
                        pe.wait_ge(ey_ok, g * UNITS + (u - 1))
                    for q in range(KT):
                        for f in range(FT):
                            w = GWO[:, f, :] if u == 0 else EWO[:, u - 1, f, :]
                            last = mm(PJ[u % 2][:, q * P:(q + 1) * P], HID[:, u % 2, f, q * P:(q + 1) * P], w,
                                      start=(f == 0), stop=(f == FT - 1))
                    last.then_inc(e2_ok, 1)

                hidden(0)
                for u in range(UNITS):
                    if u + 1 < UNITS:
                        hidden(u + 1)
                    second(u)
                pe.wait_ge(fin_ok, g + 1)


def kernel(**inputs):
    import concourse.bacc as _bacc
    from concourse.bass_utils import run_bass_kernel_spmd as _run

    a = {k: np.asarray(x) for k, x in inputs.items()}
    B, S, D = a["L0_attn_x"].shape
    L = a["L0_attn_W_qkv"].shape[0]
    FT = a["L0_attn_b_ff1"].shape[1] // P
    E = a["L0_ffn_exp_bi"].shape[0]
    pos = np.arange(S - 1, -1, -1, dtype=np.float32)
    freq = (np.float32(1.0) / np.float32(10000.0) ** (np.arange(0, D, 2, dtype=np.float32) / np.float32(D))).astype(np.float32)
    ang = (pos[:, None] * freq[None, :]).astype(np.float32)
    enc = np.concatenate([np.sin(ang), np.cos(ang)], axis=-1).astype(np.float32)
    g = lambda n: a["L0_" + n]
    arrays = [
        g("attn_x"), g("attn_W_qkv"), g("attn_W_r"), g("attn_W_o"),
        g("attn_u").reshape(-1, P).T, g("attn_v").reshape(-1, P).T,
        g("attn_ln1_g"), g("attn_ln1_b"), g("attn_W_ff1"), g("attn_b_ff1").reshape(L, FT, P).transpose(0, 2, 1),
        g("attn_W_ff2"), g("attn_b_ff2"), g("attn_ln2_g"), g("attn_ln2_b"),
        g("ffn_gate_wi"), g("ffn_gate_bi").reshape(FT, P).T, g("ffn_gate_wo"), g("ffn_gate_bo"),
        g("ffn_exp_wi"), g("ffn_exp_bi").reshape(E, FT, P).transpose(2, 0, 1), g("ffn_exp_wo"), g("ffn_exp_bo"),
        g("c").T, g("wmod"), enc.T,
    ]
    nc = _bacc.Bacc("TRN2", target_bir_lowering=False, num_devices=1)
    sent, args = {}, []
    for i, x in enumerate(arrays):
        x = np.ascontiguousarray(x)
        sent[f"in_{i}"] = x
        args.append(nc.dram_tensor(f"in_{i}", x.shape, mybir.dt.from_np(x.dtype), kind="ExternalInput").ap())
    args.append(nc.dram_tensor("out", (B, S, D), F32, kind="ExternalOutput").ap())
    adaln_block(nc, *args)
    r = _run(nc, [sent], core_ids=[0])
    return r.results[0]["out"]
```

```python
from contextlib import ExitStack

import numpy as np

import concourse.bass as bass
from concourse import mybir

F32 = mybir.dt.float32
F32R = mybir.dt.float32r
U32 = mybir.dt.uint32
ALU = mybir.AluOpType
ACT = mybir.ActivationFunctionType
AX_X = mybir.AxisListType.X

P = 128
EPS = 1e-5
SELU_SCALE = 1.0507009873554805
SELU_ALPHA = 1.6732632423543772


def wait_alone(engine, signal, value):
    engine.wait_ge(signal, value)
    engine.nop(nofuse=True)


def places(fills, first_bank):
    on, found = [0, 0], {}
    for n, key in enumerate(fills):
        bank = (n + first_bank) % 2
        on[bank] += 1
        found[key] = (n + 1, bank, on[bank])
    return found, on


def adaln_block(nc, x_d, wqkv_d, wr_d, wo_d, u_d, uv_d, ln1g_d, ln1b_d, wf1_d, bf1_d, wf2_d, bf2_d, ln2g_d, ln2b_d,
                gwi_d, gbi_d, gwo_d, gbo_d, ewi_d, ebi_d, ewo_d, ebo_d, c_d, wmod_d, rt_d, out_d):
    B, S, D = x_d.shape
    L, _, QKV = wqkv_d.shape
    HD = QKV // 3
    DH = 64
    PAIRS = HD // P
    DF = wf1_d.shape[2]
    FT = DF // P
    E = ewi_d.shape[0]
    KT = S // P
    NT = B * KT
    STEPS = PAIRS * 2 * KT
    QS = DH ** -0.5
    TPP = 2 * KT
    LAG = 3

    LAST = PAIRS - 1
    fill_at = {("o", 0): 11, ("h1", 0): 28, ("f2", 0): 37, ("h2", 0): 52}
    fill_at |= {("f1", f): t for f, t in enumerate((29, 30, 35, 36))}
    for p in range(PAIRS):
        fill_at |= {("q", p + 1): p * TPP + (p == LAST), ("k", p + 1): p * TPP + 2, ("v", p + 1): p * TPP + TPP - 1 - (p == LAST - 1)}
    at_step = {t: key for key, t in fill_at.items()}
    PARTS = {"o": 4, "f2": 1}
    FINISH = {t: n for n, t in enumerate((15, 16, 18, 20, 22, 23, 38, 39, 40, 42, 44, 47, 48))}
    VAR = [t for t, n in FINISH.items() if n in (2, 8)]
    HTC_AT = LAST * TPP - 1
    FIRST, FIRST_ON = places([("kr", i) for i in range(L * PAIRS)] + [("c", 0), ("q", 0), ("k", 0), ("v", 0)], 0)
    BODY, BODY_ON = places(sorted(fill_at, key=fill_at.get), len(FIRST) % 2)
    END, END_ON = places([("o", 0), ("h1", 0)] + [("f1", f) for f in range(FT)] + [("f2", 0), ("h2", 0)], 0)
    FILLS = len(BODY)
    ITEMS = L * B
    assert len(at_step) == len(fill_at) and FILLS % 2 == 0 and len(FIRST) % 2 == 0 and PAIRS % 2 == 0
    assert B & (B - 1) == 0 and L & (L - 1) == 0 and FT == 4
    LOG_B = B.bit_length() - 1
    UNITS = E + 1
    LNP = 5
    LOADS_O = 9
    HEADS = 2 * PAIRS
    CS = 4

    ctx = ExitStack()
    with ctx:
        def sb(name, shape, dt=F32):
            return ctx.enter_context(nc.sbuf_tensor(name, shape, dt))

        def ps(name):
            return ctx.enter_context(nc.psum_tensor(name, [P, 512], F32))

        def sem(name):
            return ctx.enter_context(nc.semaphore(name))

        X = sb("X", [P, NT * D])
        H = sb("H", [P, (B + 1) * KT * D])
        HT = sb("HT", [P, (B + 1) * S])
        HTC = sb("HTC", [P, S])
        MOD = sb("MOD", [P, B, 3 * D])
        CT = sb("CT", [P, B])
        CE = sb("CE", [P, B])
        CB = sb("CB", [P, B, P])
        WM = sb("WM", [P, 6 * D])
        WQKV = sb("WQKV", [P, QKV])
        WO = sb("WO", [P, PAIRS, D])
        WF1 = sb("WF1", [P, DF])
        WF2 = sb("WF2", [P, FT, D])
        BF1 = sb("BF1", [P, FT])
        LN = sb("LN", [P, LNP, D])
        U = sb("U", [P, PAIRS])
        RT = sb("RT", [P, S])
        ident = sb("ident", [P, P])
        Q1 = sb("Q1", [P, 2, 2, S], F32R)
        K1 = sb("K1", [P, 2, 2, S], F32R)
        K2 = sb("K2", [P, 2, 2, S], F32R)
        KR = sb("KR", [P, PAIRS, S])
        KS = sb("KS", [P, S])
        WC = sb("WC", [P, L, HEADS])
        CR = sb("CR", [P, CS, S])
        VV = sb("VV", [P, 2, KT, P])
        PR = sb("PR", [P, 4, S])
        PT = sb("PT", [P, 2, 2, KT, S])
        VEC = sb("VEC", [P, PAIRS, S])
        F = sb("F", [P, FT, S])
        Y = sb("Y", [P, KT, D])
        Z = sb("Z", [P, KT, D])
        YT = sb("YT", [P, S])
        ST = sb("ST", [P, NT, 6])
        MV = sb("MV", [P, NT, 2])
        VE = sb("VE", [P, NT])
        RS = sb("RS", [P, NT])
        HALF = sb("HALF", [P, NT])
        MIN = sb("MIN", [P, 8])
        SUM = sb("SUM", [P, 8])
        RC = sb("RC", [P, 8])
        EWO = VEC[:, :, :].rearrange("p a b -> p (a b)").rearrange("p (e f d) -> p e f d", e=E, f=FT)
        HID = PT[:, 0].rearrange("p a b c -> p (a b c)").rearrange("p (s f n) -> p s f n", s=2, f=FT)
        EWI = KR[:, :, :].rearrange("p a b -> p (a b)").rearrange("p (e f) -> p e f", e=E)
        late = PT[:, 1].rearrange("p a b c -> p (a b c)")
        GWI = late[:, 0:DF]
        GWO = late[:, DF:DF + FT * D].rearrange("p (f d) -> p f d", f=FT)
        at = DF + FT * D
        EBO = late[:, at:at + E * D].rearrange("p (e d) -> p e d", e=E)
        at += E * D
        GBO = late[:, at:at + D]
        GBI = late[:, at + D:at + D + FT]
        at += D + FT
        EBI = late[:, at:at + E * FT].rearrange("p (e f) -> p e f", e=E)
        WR = VEC[:, :, :].rearrange("p a b -> p (a b)").rearrange("p (l n) -> p l n", l=L)
        KRS = PT[:, :].rearrange("p s h k n -> p (s h k n)").rearrange("p (l a n) -> p l a n", l=2, a=PAIRS)
        UV = CR[:, :, :].rearrange("p a b -> p (a b)").rearrange("p (a b) -> p a b", a=2)
        WRV = PR[:, :, :].rearrange("p a b -> p (a b)")[:, 0:HD]
        TERMS = F[0:L * HEADS, 0, :]
        EX = PR
        RL = F
        ACC = Z
        TOP = sb("TOP", [P, KT, 8])
        TIX = sb("TIX", [P, KT, 8], U32)
        TIF = sb("TIF", [P, KT, 8])
        W12 = sb("W12", [P, KT, 2, E])
        WS = sb("WS", [P, KT, 2])
        WG = sb("WG", [P, KT, E])
        IOTA = sb("IOTA", [P, E])

        SB = [ps(f"SB{i}") for i in range(3)]
        TB = [ps(f"TB{i}") for i in range(2)]
        PVB = ps("PVB")
        PJ = [ps(f"PJ{i}") for i in range(2)]
        FB = [SB[0], SB[1], SB[2], PVB]

        ld_x, ld_c, ld_k, ld_moe, ld_ewo = (sem(n) for n in ("ld_x", "ld_c", "ld_k", "ld_moe", "ld_ewo"))
        ld_w = [sem(f"w{i}") for i in range(3)]
        ld_r = sem("ld_r")
        ld_kr = [sem(f"kr{i}") for i in range(2)]
        ld_o = sem("ld_o")
        ident_ok = sem("ident_ok")
        dve_ok = sem("dve_ok")
        var_ok, rstd_ok = sem("var_ok"), sem("rstd_ok")
        exp_c, cb_ok, mod_ok, mod_in = sem("exp_c"), sem("cb_ok"), sem("mod_ok"), sem("mod_in")
        norm_ok, tr_ok, tr_in = sem("norm_ok"), sem("tr_ok"), sem("tr_in")
        wc_ok, htc_ok = sem("wc_ok"), sem("htc_ok")
        qh_ok, kh_ok, k_ok = sem("qh_ok"), sem("kh_ok"), sem("k_ok")
        c_out = sem("c_out")
        c_in = [sem(f"c{i}_in") for i in range(CS)]
        kr_out = [sem(f"kr_out{i}") for i in range(2)]
        terms_d = nc.dram_tensor("key_terms", [L, HEADS, S], F32).ap()
        kr_d = nc.dram_tensor("keys_of_positions", [L, P, PAIRS, S], F32).ap()
        fill_ok = sem("fill_ok")
        bank_in = [sem(f"bank{i}_in") for i in range(2)]
        score_ok, min_ok, exp_ok, rec_ok, prob_ok = (sem(n) for n in ("score_ok", "min_ok", "exp_ok", "rec_ok", "prob_ok"))
        pt_ok, pv_ok, vec_in = sem("pt_ok"), sem("pv_ok"), sem("vec_in")
        pt_in = [sem(f"pt{i}_in") for i in range(2)]
        h1_ok, h2_ok = sem("h1_ok"), sem("h2_ok")
        e1_ok, ee_ok, er_ok, et_ok, eh_ok, e2_ok, ey_ok, fin_ok, st_out = (
            sem(n) for n in ("e1_ok", "ee_ok", "er_ok", "et_ok", "eh_ok", "e2_ok", "ey_ok", "fin_ok", "st_out"))

        def fills_before(it):
            return it * FILLS + len(FIRST)

        def on_bank_before(k, it):
            return it * (FILLS // 2) + (FIRST_ON[k] + 1)

        def item_before(it):
            return ((it + (B - 1)) & (B - 1)) + (it < 1)

        def on_act(key):
            return key[0] in ("kr", "q", "c", "h1", "h2") or key[0] == "f1" and key[1] < FT - 1

        def score_bank(t):
            return SB[1 if t == STEPS - 1 else t % 3]

        def bank_age(t):
            return next(n for n in range(1, STEPS) if score_bank((t - n) % STEPS) is score_bank(t))

        def pt_on_act(t):
            return t % TPP in (1, 2, 3, 4, 6, 7)

        def pt_of(t):
            p, r = divmod((t - LAG) % STEPS, TPP)
            h, q = divmod(r, KT)
            return PT[:, p % 2, h, :, q * P:(q + 1) * P]

        TAIL = range(STEPS, STEPS + LAG)

        block = ctx.enter_context(nc.Block())

        @block.sync
        def _(sp):
            xt = x_d.rearrange("b (t p) d -> p (b t) d", p=P)
            ot = out_d.rearrange("b (t p) d -> p b t d", p=P)
            sp.dma_start(CT[:, :], c_d).then_inc(ld_c, 16)
            sp.dma_start(WM[:, :], wmod_d).then_inc(ld_c, 16)
            sp.dma_start(X[:, :].rearrange("p (t d) -> p t d", d=D), xt).then_inc(ld_x, 16)

            w_parts = (0, P), (P, 5 * P), (5 * P, HD)

            def load_w(l, i):
                n, m = w_parts[i]
                sp.dma_start(WQKV[:, :].rearrange("p (t n) -> p t n", t=3)[:, :, n:m],
                             wqkv_d[l].rearrange("d (t n) -> d t n", t=3)[:, :, n:m]).then_inc(ld_w[i], 16)

            def load_kr(l, p):
                sp.dma_start(KR[:, p, :], kr_d[l, :, p, :]).then_inc(ld_kr[p > 0], 16)

            def load_o(l):
                sp.dma_start(WO[:, :, :], wo_d[l].rearrange("(a p) d -> p a d", p=P)).then_inc(ld_o, 16)
                sp.dma_start(WF1[:, :], wf1_d[l]).then_inc(ld_o, 16)
                sp.dma_start(WF2[:, :, :], wf2_d[l].rearrange("(a p) d -> p a d", p=P)).then_inc(ld_o, 16)
                sp.dma_start(BF1[:, :], bf1_d[l]).then_inc(ld_o, 16)
                for n, row in enumerate((ln1g_d, ln1b_d, ln2g_d, ln2b_d)):
                    sp.dma_start(LN[:, n, :], row[l].partition_broadcast(P)).then_inc(ld_o, 16)
                sp.dma_start(LN[:, 4, :], bf2_d[l].partition_broadcast(P)).then_inc(ld_o, 16)

            sp.dma_start(RT[:, :], rt_d).then_inc(ld_o, 16)
            sp.dma_start(WR, wr_d.rearrange("l d n -> d l n")).then_inc(ld_r, 16)
            sp.dma_start(U[:, :], u_d).then_inc(ld_k, 16)
            sp.dma_start(UV, uv_d.rearrange("a n -> (a n)").partition_broadcast(P).rearrange("p (a n) -> p a n", a=2)
                         ).then_inc(ld_k, 16)
            for i in range(3):
                load_w(0, i)
            load_o(0)

            half = PAIRS // 2
            for l in range(L):
                for a in range(0, PAIRS, half):
                    for i in (a + half - 2, a + half - 1):
                        _, k, m = FIRST["kr", l * PAIRS + i]
                        sp.wait_ge(bank_in[k], m + 1)
                    sp.dma_start(kr_d[l, :, a:a + half, :], KRS[:, l % 2, a:a + half, :]).then_inc(kr_out[l % 2], 16)
                if l == 1:
                    sp.wait_ge(kr_out[0], 32)
                    for p in range(PAIRS):
                        load_kr(0, p)
            _, k, m = FIRST["c", 0]
            sp.wait_ge(bank_in[k], m + 1)
            sp.dma_start(terms_d.rearrange("l h s -> (l h) s"), TERMS).then_inc(c_out, 16)
            sp.wait_ge(c_out, 16)

            def load_terms(l, it, after={}):
                tiles = sp.snap(it * STEPS)
                for h in range(HEADS):
                    wait_alone(sp, min_ok, tiles + (h + 1) * KT)
                    sp.dma_start(CR[:, h % CS, :], terms_d[l, h].partition_broadcast(P)).then_inc(c_in[h % CS], 16)
                    if h in after:
                        after[h]()

            def next_first(l, it):
                wait_alone(sp, fill_ok, fills_before(it))
                load_w(l, 0)
                wait_alone(sp, bank_in[BODY["k", PAIRS][1]], on_bank_before(BODY["k", PAIRS][1], it))
                load_kr(l, 0)

            def next_kr(l, it, p):
                _, k, m = BODY["k", p]
                wait_alone(sp, bank_in[k], on_bank_before(k, it) + m)
                load_kr(l, p)

            def next_w(l, it, i):
                wait_alone(sp, fill_ok, fills_before(it) + BODY["v", (4, LAST)[i - 1]][0])
                load_w(l, i)

            for i in range(2):
                sp.wait_ge(kr_out[i], 16 * L)
            with sp.Fori(0, L) as l:
                it = sp.snap(l * B)
                load_terms(l, it)
                _, k, m = BODY["h2", 0]
                wait_alone(sp, bank_in[k], on_bank_before(k, it) + m)
                load_o(l)
                with sp.Fori(1, B - 1) as b:
                    load_terms(l, l * B + b)
                it = sp.snap(l * B + (B - 1))
                nl = sp.snap((l + 1) & (L - 1))
                after = {CS - 1: lambda: next_first(nl, it), 10: lambda: (next_kr(nl, it, 4), next_w(nl, it, 1))}
                after |= {2 * p + 2: lambda p=p: next_kr(nl, it, p) for p in (1, 2, 3, 5, 6)}
                load_terms(l, it, after)
                next_w(nl, it, 2)
                next_kr(nl, it, LAST)
            sp.wait_ge(ld_kr[0], 16 * (L + 1))
            sp.wait_ge(ld_kr[1], 16 * (PAIRS - 1) * (L + 1))
            sp.wait_ge(fill_ok, fills_before(ITEMS) + END["o", 0][0])
            for dst, src in ((GWI, gwi_d), (GWO, gwo_d.rearrange("(a p) d -> p a d", p=P)), (GBI, gbi_d),
                             (EBI, ebi_d), (GBO, gbo_d.partition_broadcast(P)),
                             (EBO, ebo_d.rearrange("e d -> (e d)").partition_broadcast(P).rearrange("p (e d) -> p e d", e=E))):
                sp.dma_start(dst, src).then_inc(ld_moe, 16)
            sp.dma_start(EWI, ewi_d.rearrange("e p f -> p e f")).then_inc(ld_ewo, 16)
            for e in range(E):
                sp.dma_start(EWO[:, e], ewo_d[e].rearrange("(a p) d -> p a d", p=P)).then_inc(ld_ewo, 16)
            for g in range(B):
                sp.wait_ge(fin_ok, g + 1)
                sp.dma_start(ot[:, g], X[:, g * S:(g + 1) * S].rearrange("p (t d) -> p t d", d=D)).then_inc(st_out, 16)
            sp.wait_ge(st_out, 16 * B)

        @block.gpsimd
        def _(pool):
            nc.gpsimd.memset(ident[:, :], 0.0).then_inc(ident_ok, 1)
            pool.wait_ge(ident_ok, 1)
            nc.gpsimd.affine_select(out=ident[:, :], in_=ident[:, :], compare_op=ALU.not_equal, fill=1.0, base=0,
                                    pattern=[[-1, P]], channel_multiplier=1).then_inc(ident_ok, 1)
            nc.gpsimd.iota(IOTA[:, :], [[1, E]], base=0, channel_multiplier=0,
                           allow_small_or_imprecise_dtypes=True).then_inc(ident_ok, 1)
            nc.gpsimd.memset(HALF[:, :], -0.5).then_inc(ident_ok, 1)
            pool.wait_ge(ident_ok, 4)

            def rstd(n, tiles):
                pool.wait_ge(var_ok, n)
                nc.gpsimd.tensor_tensor(RS[:, 0:tiles], VE[:, 0:tiles], HALF[:, 0:tiles], ALU.pow).then_inc(rstd_ok, 1)

            rstd(1, NT)
            with pool.Fori(0, ITEMS) as it:
                tiles = pool.snap(it * STEPS)
                for t in range(STEPS):
                    wait_alone(pool, rec_ok, tiles + (t + 2))
                    pr = PR[:, t % 4, :]
                    nc.gpsimd.tensor_scalar(pr, pr, RC[:, t % 8:t % 8 + 1], 1.0, ALU.mult, ALU.mult).then_inc(prob_ok, 1)
                    if t + 1 in VAR:
                        rstd(it * 2 + 2 + VAR.index(t + 1), KT)
            rstd(2 * L * B + 2, KT)
            rstd(2 * L * B + 3, KT)
            rstd(2 * L * B + 4, NT)
        @block.scalar
        def _(act):
            act.wait_ge(ld_c, 32)
            nc.scalar.activation(CE[:, :], CT[:, :], ACT.Exp, scale=-1.0).then_inc(exp_c, 1)

            def high_q(p, bank):
                c = p % PAIRS
                for h in range(2):
                    r = slice(h * DH, (h + 1) * DH)
                    nc.scalar.activation(Q1[r, p % 2, h, :], bank[r, :], ACT.Identity, bias=U[r, c:c + 1]).then_inc(qh_ok, 1)

            def high_k(p, h, table, on_bank):
                r = slice(h * DH, (h + 1) * DH)
                if h == 0:
                    _, k, m = table["k", p]
                    act.wait_ge(bank_in[k], on_bank[k] + m)
                nc.scalar.copy(K1[0:DH, p % 2, h, :], KS[r, :])
                nc.scalar.copy(K1[DH:P, p % 2, h, :], KS[r, :]).then_inc(kh_ok, 1)

            def take_v(p, bank):
                return nc.scalar.copy(VV[:, p % 2], bank[:, :].rearrange("p (t d) -> p t d", d=P))

            def take_fill(key, table, fills, slot):
                kind, p = key
                n, k, _ = table[key]
                bank = PJ[k]
                act.wait_ge(fill_ok, fills + n)
                if kind == "q":
                    high_q(p, bank)
                elif kind == "kr":
                    l = p // PAIRS
                    if l >= 2 and p % PAIRS == 0:
                        act.wait_ge(kr_out[l % 2], 32 * (l // 2))
                    nc.scalar.mul(KRS[:, l % 2, p % PAIRS, :], bank[:, :], -QS).then_inc(bank_in[k], 1)
                elif kind == "c":
                    nc.scalar.copy(TERMS, bank[0:L * HEADS, :]).then_inc(bank_in[k], 1)
                elif kind == "h1":
                    nc.scalar.copy(YT[:, :], bank[:, :]).then_inc(bank_in[k], 1)
                elif kind == "f1":
                    nc.scalar.activation(F[:, p, :], bank[:, :], ACT.Relu, bias=BF1[:, p:p + 1]).then_inc(bank_in[k], 1)
                elif kind == "h2":
                    nc.scalar.copy(HT[:, bass.ts(slot, S)], bank[:, :]).then_inc(bank_in[k], 1)

            for key in FIRST:
                if on_act(key):
                    if key == ("q", 0):
                        act.wait_ge(ld_k, 32)
                    take_fill(key, FIRST, 0, 0)
            for h in range(2):
                high_k(0, h, FIRST, [1, 1])
            for i in range(2):
                act.wait_ge(kr_out[i], 16 * L)

            def copy_pt(t, tiles):
                act.wait_ge(pt_ok, tiles + (t + 2))
                nc.scalar.copy(pt_of(t), TB[t % 2][:, :].rearrange("p (t d) -> p t d", d=P)).then_inc(pt_in[t % 2], 1)

            def take_vec(p, pairs):
                act.wait_ge(pv_ok, pairs + (p + 1))
                nc.scalar.copy(VEC[:, (p - 2) % PAIRS, :], PVB[:, :]).then_inc(vec_in, 1)

            with act.Fori(0, ITEMS) as it:
                slot = act.snap(item_before(it))
                tiles = act.snap(it * STEPS)
                pairs = act.snap(it * PAIRS)
                fills = act.snap(fills_before(it))
                on_bank = [act.snap(on_bank_before(k, it)) for k in range(2)]
                for t in range(STEPS):
                    p, r = divmod(t, TPP)
                    act.wait_ge(min_ok, tiles + (t + 1 + CS * KT))
                    act.wait_ge(pt_ok, tiles + (t + 1))
                    nc.scalar.activation(PR[:, t % 4, :], score_bank(t)[:, :], ACT.Exp, bias=MIN[:, t % 8:t % 8 + 1],
                                         scale=-1.0, accum_out=SUM[:, t % 8:t % 8 + 1]).then_inc(exp_ok, 1)
                    if pt_on_act(t):
                        copy_pt(t, tiles)
                    if r == 0:
                        n, k, _ = BODY["v", p] if p else (0, BODY["v", PAIRS][1], 0)
                        act.wait_ge(fill_ok, fills + n)
                        take_v(p, PJ[k]).then_inc(bank_in[k], 1)
                    if t in at_step and on_act(at_step[t]):
                        take_fill(at_step[t], BODY, fills, slot)
                    if r in (4, 5):
                        high_k(p + 1, r - 4, BODY, on_bank)
                    if r == 1:
                        take_vec(p, pairs)
            for t in TAIL:
                if pt_on_act(t):
                    copy_pt(t, (ITEMS - 1) * STEPS)
            n, k, _ = BODY["v", PAIRS]
            act.wait_ge(fill_ok, fills_before(ITEMS))
            take_v(PAIRS, PJ[k]).then_inc(bank_in[k], 1)
            take_vec(0, ITEMS * PAIRS)
            take_vec(1, ITEMS * PAIRS)
            for key in END:
                if on_act(key):
                    take_fill(key, END, fills_before(ITEMS), B - 1)
            act.wait_ge(ld_moe, 16 * 6)
            with act.Fori(0, B) as g:
                tiles = act.snap(g * (UNITS * FT))
                for j in range(UNITS * FT):
                    u, f = divmod(j, FT)
                    bias = GBI[:, f:f + 1] if u == 0 else EBI[:, u - 1, f:f + 1]
                    act.wait_ge(e1_ok, tiles + (j + 1))
                    act.wait_ge(eh_ok, tiles + (j + 1))
                    nc.scalar.activation(EX[:, j % 4, :], FB[j % 4][:, :], ACT.Exp, bias=bias).then_inc(ee_ok, 1)
                    nc.scalar.activation(RL[:, j % 4, :], FB[j % 4][:, :], ACT.Relu, bias=bias).then_inc(er_ok, 1)

        @block.vector
        def _(dve):
            v = nc.vector

            def norm_stats(src, tiles, link, n):
                for t in range(tiles):
                    last = v.bn_stats(ST[:, t, :], src[:, t * D:(t + 1) * D])
                link(last)
                for t in range(tiles):
                    last = v.bn_aggr(MV[:, t, :], ST[:, t, :])
                link(last)
                v.tensor_scalar(VE[:, 0:tiles], MV[:, 0:tiles, 1], EPS, None, ALU.add).then_inc(var_ok, 1)
                wait_alone(dve, rstd_ok, n)

            def normalise(dst, src, tiles, link):
                for t in range(tiles):
                    last = v.tensor_scalar(dst[:, t * D:(t + 1) * D], src[:, t * D:(t + 1) * D], MV[:, t, 0:1],
                                           RS[:, t:t + 1], ALU.subtract, ALU.mult)
                link(last)

            def row(ap):
                return ap.unsqueeze(1).to_broadcast([P, KT, D])

            def tk(ap):
                return ap.rearrange("p (t d) -> p t d", d=D)

            def chain(base):
                n = [0]

                def link(ins):
                    n[0] += 1
                    ins.then_inc(dve_ok, 1)
                    if isinstance(base, int):
                        dve.wait_ge(dve_ok, base + n[0])
                    else:
                        wait_alone(dve, dve_ok, base + n[0])
                return link, n

            link, n0 = chain(0)
            dve.wait_ge(exp_c, 1)
            link(v.tensor_scalar(CE[:, :], CE[:, :], 1.0, None, ALU.add))
            link(v.reciprocal(CE[:, :], CE[:, :]))
            link(v.tensor_tensor(CE[:, :], CE[:, :], CT[:, :], ALU.mult))
            v.tensor_copy(CB[:, :, :], CE[:, :].unsqueeze(2).to_broadcast([P, B, P])).then_inc(cb_ok, 1)

            def take_mod(n):
                for b in range(B):
                    dve.wait_ge(mod_ok, n * B + b + 1)
                    last = v.tensor_copy(MOD[:, b, :], PJ[b % 2][:, 0:3 * D])
                    last.then_inc(mod_in, 1)
                dve.wait_ge(mod_in, (n + 1) * B)

            def modulated(n, link):
                norm_stats(X, NT, link, n)
                normalise(H, X, NT, link)
                for b in range(B):
                    h = tk(H[:, b * S:(b + 1) * S])
                    last = v.scalar_tensor_tensor(out=h, in0=row(MOD[:, b, D:2 * D]), scalar=1.0, in1=h,
                                                  op0=ALU.add, op1=ALU.mult)
                link(last)
                for b in range(B):
                    h = tk(H[:, b * S:(b + 1) * S])
                    v.tensor_tensor(h, h, row(MOD[:, b, 0:D]), ALU.add).then_inc(norm_ok, 1)

            def take_transposed(n):
                for b in range(B):
                    dve.wait_ge(tr_ok, n * B + b + 1)
                    v.tensor_copy(HT[:, b * S:(b + 1) * S], TB[b % 2][:, :]).then_inc(tr_in, 1)

            def signed_gate(link):
                g = MOD[:, :, 2 * D:3 * D]
                a, s = tk(Y[:, :, :].rearrange("p a b -> p (a b)")), tk(Z[:, :, :].rearrange("p a b -> p (a b)"))
                link(v.scalar_tensor_tensor(out=a, in0=g, scalar=-1.0, in1=g, op0=ALU.mult, op1=ALU.max))
                link(v.tensor_scalar(a, a, 0.25, None, ALU.max))
                link(v.tensor_scalar(s, g, 0.0, 2.0, ALU.is_ge, ALU.mult))
                link(v.scalar_tensor_tensor(out=g, in0=s, scalar=-1.0, in1=a, op0=ALU.add, op1=ALU.mult))

            take_mod(0)
            dve.sem_inc(bank_in[0], 1)
            dve.sem_inc(bank_in[1], 1)
            dve.wait_ge(ld_k, 32)
            link(v.tensor_tensor(UV[:, 1, :], UV[:, 1, :], UV[:, 0, :], ALU.subtract))
            link(v.tensor_scalar(UV[:, 1, :], UV[:, 1, :], -QS, None, ALU.mult))
            dve.wait_ge(ld_r, 16)
            for l in range(L):
                link(v.tensor_tensor(WRV, WR[:, l, :], UV[:, 1, :], ALU.mult))
                link(v.tensor_reduce(WC[:, l, :], WRV.rearrange("p (h e) -> p h e", e=DH), AX_X, ALU.add))
            v.tensor_copy(UV[:, 0, 0:1], UV[:, 1, 0:1]).then_inc(wc_ok, 1)
            dve.wait_ge(ld_x, 16)
            modulated(1, link)
            take_transposed(0)
            dve.wait_ge(tr_in, B)
            v.tensor_copy(HTC[:, :], HT[:, 0:S])
            v.memset(H[:, B * S:(B + 1) * S], 0.0)
            v.memset(PR[:, :, :].rearrange("p a b -> p (a b)"), 0.0)
            v.memset(SUM[:, :], 1.0)
            v.memset(VV[:, 1, :, :].rearrange("p a b -> p (a b)"), 0.0)
            for h in range(2):
                v.memset(K2[DH - h * DH:P - h * DH, :, h, :].bitcast(F32), 0.0)
            v.memset(PVB[:, :], 0.0)
            v.memset(RC[:, :], 0.0).then_inc(htc_ok, 1)
            dve.wait_ge(htc_ok, 1)
            for signal, n in ((pv_ok, 1), (pt_ok, 1), (pt_in[0], 1), (pt_in[1], 1), (exp_ok, 4), (prob_ok, LAG)):
                dve.sem_inc(signal, n)
            dve.sem_inc(min_ok, CS * KT)
            signed_gate(link)
            before = n0[0]

            LINKS = 9
            y, z = Y[:, :, :].rearrange("p a b -> p (a b)"), Z[:, :, :].rearrange("p a b -> p (a b)")

            def finish(n, it, slot, link, table, fills):
                def bank_of(key):
                    m, k, _ = table[key]
                    dve.wait_ge(fill_ok, fills + m)
                    return PJ[k], bank_in[k]

                if n == 0:
                    bank, free = bank_of(("o", 0))
                    v.tensor_tensor(y, bank[:, :], H[:, bass.ts(slot, S)], ALU.add).then_inc(free, 1)
                    wait_alone(dve, free, bank_total(table, ("o", 0)))
                elif n in (1, 7):
                    for t in range(KT):
                        last = v.bn_stats(ST[:, t, :], (y, z)[n == 7][:, t * D:(t + 1) * D])
                    link(last)
                elif n in (2, 8):
                    for t in range(KT):
                        last = v.bn_aggr(MV[:, t, :], ST[:, t, :])
                    link(last)
                    v.tensor_scalar(VE[:, 0:KT], MV[:, 0:KT, 1], EPS, None, ALU.add).then_inc(var_ok, 1)
                elif n in (3, 9):
                    wait_alone(dve, rstd_ok, it * 2 + (2 if n == 3 else 3))
                    normalise(*((y, y) if n == 3 else (z, z)), KT, link)
                elif n == 4:
                    link(v.tensor_tensor(tk(y), tk(y), row(LN[:, 0, :]), ALU.mult))
                elif n == 5:
                    v.tensor_tensor(tk(y), tk(y), row(LN[:, 1, :]), ALU.add).then_inc(h1_ok, 1)
                elif n == 6:
                    bank, free = bank_of(("f2", 0))
                    v.tensor_tensor(tk(z), tk(bank[:, :]), row(LN[:, 4, :]), ALU.add).then_inc(free, 1)
                    wait_alone(dve, free, bank_total(table, ("f2", 0)))
                elif n == 10:
                    link(v.tensor_tensor(tk(z), tk(z), row(LN[:, 2, :]), ALU.mult))
                elif n == 11:
                    v.tensor_tensor(tk(z), tk(z), row(LN[:, 3, :]), ALU.add).then_inc(h2_ok, 1)
                elif n == 12:
                    wait_alone(dve, h2_ok, it + 1)
                    link(v.tensor_copy(H[:, bass.ts(slot, S)], z))

            def low_q(p, h, table, pairs):
                _, k, _ = table["q", p]
                c = p % PAIRS
                r, o = slice(h * DH, (h + 1) * DH), slice(DH - h * DH, P - h * DH)
                dve.wait_ge(qh_ok, pairs * 2 + (2 * p + h + 1))
                ins = v.scalar_tensor_tensor(out=Q1[o, p % 2, h, :], in0=PJ[k][r, :], scalar=U[r, c:c + 1],
                                             in1=Q1[r, p % 2, h, :].bitcast(F32), op0=ALU.add, op1=ALU.subtract)
                if h == 1:
                    ins.then_inc(bank_in[k], 1)

            def sum_k(p, table, fills, layers):
                n, k, m = table["k", p]
                if p in (0, 1, PAIRS):
                    i = p == 1
                    wait_alone(dve, ld_kr[i], layers * (16 * (1, PAIRS - 1)[i]))
                wait_alone(dve, fill_ok, fills + n)
                v.scalar_tensor_tensor(out=KS[:, :], in0=PJ[k][:, :], scalar=-QS, in1=KR[:, p % PAIRS, :], op0=ALU.mult,
                                       op1=ALU.add).then_inc(bank_in[k], 1)

            def low_k(p, h, pairs):
                r = slice(h * DH, (h + 1) * DH)
                dve.wait_ge(kh_ok, pairs * 2 + (2 * p + h + 1))
                ins = v.tensor_tensor(K2[r, p % 2, h, :], KS[r, :], K1[r, p % 2, h, :].bitcast(F32), ALU.subtract)
                if h == 1:
                    ins.then_inc(k_ok, 1)

            def take_relu(f, table, fills):
                m, k, _ = table["f1", f]
                dve.wait_ge(fill_ok, fills + m)
                v.tensor_scalar(F[:, f, :], PJ[k][:, :], BF1[:, f:f + 1], 0.0, ALU.add, ALU.max).then_inc(bank_in[k], 1)

            for h in range(2):
                low_q(0, h, FIRST, 0)
            sum_k(0, FIRST, 0, 1)
            for h in range(2):
                low_k(0, h, 0)
            for i in range(2):
                dve.wait_ge(kr_out[i], 16 * L)

            def reciprocal(t, tiles):
                dve.wait_ge(exp_ok, tiles + (t + 4))
                s = (t - 1) % 8
                v.reciprocal(RC[:, s:s + 1], SUM[:, s:s + 1]).then_inc(rec_ok, 1)

            def copy_pt(t, tiles):
                dve.wait_ge(pt_ok, tiles + (t + 2))
                v.tensor_copy(pt_of(t), TB[t % 2][:, :].rearrange("p (t d) -> p t d", d=P)).then_inc(pt_in[t % 2], 1)

            with dve.Fori(0, ITEMS) as it:
                slot = dve.snap(item_before(it))
                after = dve.snap((it + 1) & (B - 1))
                tiles = dve.snap(it * STEPS)
                fills = dve.snap(fills_before(it))
                pairs = dve.snap(it * PAIRS)
                layers = dve.snap((it >> LOG_B) + 1)
                next_layers = dve.snap(((it + 1) >> LOG_B) + 1)
                links = dve.snap(it * LINKS + before)
                link, n1 = chain(links)

                def bank_total(table, key):
                    return on_bank_before(table[key][1], it) + table[key][2]

                for t in range(STEPS):
                    p, r = divmod(t, TPP)
                    h = t // KT
                    if t % KT == 0:
                        wait_alone(dve, c_in[h % CS], it * (HEADS // CS * 16) + (h // CS + 1) * 16)
                    wait_alone(dve, score_ok, tiles + (t + 1))
                    s = score_bank(t)[:, :]
                    v.tensor_tensor_reduce(out=s, in0=s, in1=CR[:, h % CS, :], scale=1.0, scalar=3e38, op0=ALU.add,
                                           op1=ALU.min, accum_out=MIN[:, t % 8:t % 8 + 1]).then_inc(min_ok, 1)
                    reciprocal(t, tiles)
                    if not pt_on_act(t):
                        copy_pt(t, tiles)
                    for h in range(2):
                        if fill_at["q", p + 1] == t - 1 - h:
                            low_q(p + 1, h, BODY, pairs)
                    if r == 3:
                        sum_k(p + 1, BODY, fills, layers if p < LAST else next_layers)
                    if r in (5, 6):
                        low_k(p + 1, r - 5, pairs)
                    if t in FINISH:
                        finish(FINISH[t], it, slot, link, BODY, fills)
                    if t in at_step and at_step[t][0] == "f1" and not on_act(at_step[t]):
                        take_relu(at_step[t][1], BODY, fills)
                    if t == HTC_AT:
                        dve.wait_ge(fill_ok, fills + BODY["v", LAST][0])
                        _, k, _ = BODY["h2", 0]
                        wait_alone(dve, bank_in[k], bank_total(BODY, ("h2", 0)))
                        v.tensor_copy(HTC[:, :], HT[:, bass.ts(after, S)]).then_inc(htc_ok, 1)
                assert n1[0] == LINKS, n1
            reciprocal(STEPS, (ITEMS - 1) * STEPS)
            for t in TAIL:
                if not pt_on_act(t):
                    copy_pt(t, (ITEMS - 1) * STEPS)
            def add_branch(b):
                x, branch = tk(X[:, b * S:(b + 1) * S]), tk(H[:, b * S:(b + 1) * S])
                link(v.tensor_tensor(branch, branch, row(MOD[:, b, 2 * D:3 * D]), ALU.mult))
                return v.tensor_tensor(x, x, branch, ALU.add)

            link, n1 = chain(ITEMS * LINKS + before)
            for b in range(B - 1):
                add_branch(b)
            end = (ITEMS + 1) * LINKS + before + B - 1

            def bank_total(table, key):
                return on_bank_before(table[key][1], ITEMS) + table[key][2]

            for n in range(6):
                finish(n, L * B, B - 1, link, END, fills_before(ITEMS))
            for f in (FT - 1,):
                take_relu(f, END, fills_before(ITEMS))
            for n in range(6, 13):
                finish(n, L * B, B - 1, link, END, fills_before(ITEMS))

            link, n2 = chain(end)
            dve.wait_ge(dve_ok, end)
            link(add_branch(B - 1))
            take_mod(1)
            modulated(2 * L * B + 4, link)
            take_transposed(1)
            dve.wait_ge(tr_in, 2 * B)
            signed_gate(link)
            before2 = end + n2[0]

            dve.wait_ge(ld_moe, 16 * 6)
            dve.wait_ge(ident_ok, 4)
            for signal, n in ((er_ok, 4), (eh_ok, 4), (ey_ok, 1)):
                dve.sem_inc(signal, n)
            TILES = UNITS * FT
            y, acc = Y[:, :, :], ACC[:, :, :]
            GLINKS = 8 + UNITS - 1
            with dve.Fori(0, B) as g:
                tiles = dve.snap(g * TILES)
                links = dve.snap(g * GLINKS + before2)
                link, n3 = chain(links)

                def capped(j):
                    dve.wait_ge(ee_ok, tiles + (j + 1))
                    e = EX[:, j % 4, :]
                    v.tensor_scalar(e, e, 1.0, -1.0, ALU.min, ALU.add).then_inc(et_ok, 1)

                def selu(j):
                    u, f = divmod(j, FT)
                    if u >= 2 and f == 0:
                        dve.wait_ge(e2_ok, g * UNITS + (u - 1))
                    wait_alone(dve, et_ok, tiles + (j + 1))
                    dve.wait_ge(er_ok, tiles + (j + 5))
                    v.scalar_tensor_tensor(out=HID[:, u % 2, f, :], in0=EX[:, j % 4, :], scalar=SELU_ALPHA,
                                           in1=RL[:, j % 4, :], op0=ALU.mult, op1=ALU.add).then_inc(eh_ok, 1)

                def top2():
                    for t in range(KT):
                        last = v.max(TOP[:, t, :], Y[:, t, :])
                    link(last)
                    for t in range(KT):
                        last = v.max_index(TIX[:, t, :], TOP[:, t, :], Y[:, t, :])
                    link(last)
                    v.tensor_copy(TIF[:, :, :], TIX[:, :, :])
                    link(v.tensor_tensor(WS[:, :, 0:1], TOP[:, :, 0:1], TOP[:, :, 1:2], ALU.add))
                    link(v.reciprocal(WS[:, :, 1:2], WS[:, :, 0:1]))
                    link(v.tensor_tensor(TOP[:, :, 0:2], TOP[:, :, 0:2], WS[:, :, 1:2].to_broadcast([P, KT, 2]), ALU.mult))
                    for t in range(KT):
                        for k in range(2):
                            last = v.tensor_scalar(W12[:, t, k, :], IOTA[:, :], TIF[:, t, k:k + 1], TOP[:, t, k:k + 1],
                                                   ALU.is_equal, ALU.mult)
                    link(last)
                    link(v.tensor_tensor(WG[:, :, :], W12[:, :, 0, :], W12[:, :, 1, :], ALU.add))

                def take_out(u):
                    dve.wait_ge(e2_ok, g * UNITS + (u + 1))
                    bias = GBO[:, :] if u == 0 else EBO[:, u - 1, :]
                    ins = v.scalar_tensor_tensor(out=y, in0=tk(PJ[u % 2][:, :]), scalar=SELU_SCALE, in1=row(bias),
                                                 op0=ALU.mult, op1=ALU.add)
                    ins.then_inc(ey_ok, 1)
                    wait_alone(dve, ey_ok, g * UNITS + (u + 2))
                    if u == 0:
                        top2()
                        return
                    for t in range(KT):
                        w = WG[:, t, u - 1:u]
                        if u == 1:
                            last = v.tensor_scalar(ACC[:, t, :], Y[:, t, :], w, None, ALU.mult)
                        else:
                            last = v.scalar_tensor_tensor(out=ACC[:, t, :], in0=Y[:, t, :], scalar=w,
                                                          in1=ACC[:, t, :], op0=ALU.mult, op1=ALU.add)
                    link(last)

                for j in range(TILES):
                    capped(j)
                    if j >= 1:
                        selu(j - 1)
                    if j % FT == FT - 1 and j >= 2 * FT - 1:
                        take_out(j // FT - 1)
                selu(TILES - 1)
                take_out(UNITS - 1)
                gate = MOD[:, :, :].rearrange("p b d -> p (b d)")[:, bass.ts(g * 3 + 2, D)]
                link(v.tensor_tensor(acc, acc, gate.unsqueeze(1).to_broadcast([P, KT, D]), ALU.mult))
                x = X[:, bass.ts(g, S)]
                v.tensor_tensor(x, x, ACC[:, :, :].rearrange("p a b -> p (a b)"), ALU.add).then_inc(fin_ok, 1)
                assert n3[0] == GLINKS, n3

        @block.tensor
        def _(pe):
            mm = nc.tensor.matmul

            def mod_rows(n):
                for b in range(B):
                    i = n * B + b
                    if i >= 2:
                        pe.wait_ge(mod_in, i - 1)
                    mm(PJ[b % 2][:, 0:3 * D], CB[:, b, :], WM[:, n * 3 * D:(n + 1) * 3 * D], start=True, stop=True
                       ).then_inc(mod_ok, 1)

            def transposes(bank, src, done):
                for t in range(KT):
                    last = nc.tensor.transpose(bank[:, t * P:(t + 1) * P], src[:, t * P:(t + 1) * P], ident[:, :])
                last.then_inc(done, 1)

            def transpose_all(n):
                for b in range(B):
                    pe.wait_ge(norm_ok, n * B + b + 1)
                    if b >= 2:
                        pe.wait_ge(tr_in, n * B + b - 1)
                    transposes(TB[b % 2], H[:, b * S:(b + 1) * S], tr_ok)

            pe.wait_ge(cb_ok, 1)
            pe.wait_ge(ld_c, 32)
            mod_rows(0)
            def part(key, table, fills, on_bank, i=0, parts=1):
                kind, p = key
                n, k, m = table[key]
                bank = PJ[k]
                if i == 0:
                    pe.wait_ge(bank_in[k], on_bank[k] + (m - 1))
                if kind in ("q", "k"):
                    c = (0 if kind == "q" else HD) + p % PAIRS * P
                    ins = mm(bank[:, :], WQKV[:, c:c + P], HTC[:, :], start=True, stop=True)
                elif kind == "v":
                    c = 2 * HD + p % PAIRS * P
                    for q in range(KT):
                        ins = mm(bank[:, q * P:(q + 1) * P], HTC[:, q * P:(q + 1) * P], WQKV[:, c:c + P],
                                 start=True, stop=True)
                elif kind == "kr":
                    l, p = divmod(p, PAIRS)
                    ins = mm(bank[:, :], WR[:, l, p * P:(p + 1) * P], RT[:, :], start=True, stop=True)
                elif kind == "c":
                    ins = mm(bank[0:L * HEADS, :], WC[:, :, :].rearrange("p l h -> p (l h)"), RT[:, :], start=True, stop=True)
                elif kind in ("o", "f2"):
                    if kind == "f2" and i == 0:
                        last_on = {table["f1", f][1]: table["f1", f][2] for f in range(FT)}
                        for j, c in last_on.items():
                            if j != k:
                                pe.wait_ge(bank_in[j], on_bank[j] + c)
                    src, w, tiles_k = (VEC, WO, PAIRS) if kind == "o" else (F, WF2, FT)
                    for q in range(i * KT // parts, (i + 1) * KT // parts):
                        for a in range(tiles_k):
                            ins = mm(bank[:, q * P:(q + 1) * P], src[:, a, q * P:(q + 1) * P], w[:, a, :],
                                     start=(a == 0), stop=(a == tiles_k - 1))
                    if i < parts - 1:
                        return
                elif kind in ("h1", "h2"):
                    src = (Y if kind == "h1" else Z)[:, :, :].rearrange("p a b -> p (a b)")
                    for q in range(KT):
                        ins = nc.tensor.transpose(bank[:, q * P:(q + 1) * P], src[:, q * P:(q + 1) * P], ident[:, :])
                elif kind == "f1":
                    if p == 0:
                        _, j, c = table["h1", 0]
                        pe.wait_ge(bank_in[j], on_bank[j] + c)
                    ins = mm(bank[:, :], WF1[:, p * P:(p + 1) * P], YT[:, :], start=True, stop=True)
                ins.then_inc(fill_ok, 1)

            pe.wait_ge(mod_in, B)
            pe.wait_ge(ld_o, 16)
            pe.wait_ge(ld_r, 16)
            for key in FIRST:
                if key == ("c", 0):
                    pe.wait_ge(wc_ok, 1)
                if key == ("q", 0):
                    pe.wait_ge(ident_ok, 4)
                    transpose_all(0)
                    pe.wait_ge(htc_ok, 1)
                    pe.wait_ge(ld_w[0], 16)
                part(key, FIRST, 0, [1, 1])

            def turn(t, tiles, halves):
                pe.wait_ge(prob_ok, tiles + (t + 1))
                pe.wait_ge(pt_in[t % 2], halves + (t // 2 + 1))
                transposes(TB[t % 2], PR[:, (t - LAG) % 4, :], pt_ok)

            def values(p, i, halves, pairs):
                if i == 0:
                    pe.wait_ge(pt_in[0], halves + (p * KT + LAG // 2 + 2))
                    pe.wait_ge(pt_in[1], halves + (p * KT + LAG // 2 + 1))
                    pe.wait_ge(vec_in, pairs + (p + 1))
                s = (p - 1) % 2
                for h in range(2):
                    last = mm(PVB[h * DH:(h + 1) * DH, :], VV[:, s, i, h * DH:(h + 1) * DH], PT[:, s, h, i, :],
                              start=(i == 0), stop=(i == KT - 1))
                if i == KT - 1:
                    last.then_inc(pv_ok, 1)

            with pe.Fori(0, ITEMS) as it:
                tiles = pe.snap(it * STEPS)
                halves = pe.snap(it * (STEPS // 2))
                pairs = pe.snap(it * PAIRS)
                fills = pe.snap(fills_before(it))
                on_bank = [pe.snap(on_bank_before(k, it)) for k in range(2)]
                layers = pe.snap(((it >> LOG_B) + 1) * 16)
                next_layers = pe.snap((((it + 1) >> LOG_B) + 1) * 16)
                params = pe.snap((((it + (B - 1)) >> LOG_B) + 1) * (16 * LOADS_O) + 16)
                for t in range(STEPS):
                    p, r = divmod(t, TPP)
                    h, q = divmod(r, KT)
                    if r == 0:
                        if p:
                            _, j, i = BODY["q", p]
                            pe.wait_ge(bank_in[j], on_bank[j] + i)
                        pe.wait_ge(k_ok, pairs + (p + 1))
                    pe.wait_ge(exp_ok, tiles + (t + 5 - bank_age(t)))
                    part_q = Q1[:, p % 2, h, q * P:(q + 1) * P]
                    mm(score_bank(t)[:, :], part_q, K1[:, p % 2, h, :], start=True, stop=False)
                    mm(score_bank(t)[:, :], part_q, K2[:, p % 2, h, :], start=False, stop=True).then_inc(score_ok, 1)
                    turn(t, tiles, halves)
                    if LAG < r:
                        values(p, r - LAG - 1, halves, pairs)
                    for key, start in fill_at.items():
                        parts = PARTS.get(key[0], 1)
                        if not start <= t < start + parts:
                            continue
                        if t == start:
                            if key[0] == "o":
                                pe.wait_ge(ld_o, params)
                                pe.wait_ge(vec_in, pairs + 2)
                            if key[0] == "h1":
                                pe.wait_ge(h1_ok, it + 1)
                            if key[0] == "h2":
                                pe.wait_ge(h2_ok, it + 1)
                            if key == ("q", PAIRS):
                                pe.wait_ge(htc_ok, it + 2)
                                pe.wait_ge(ld_w[0], next_layers)
                            if key == ("q", 1):
                                pe.wait_ge(ld_w[1], layers)
                            if key == ("q", 5):
                                pe.wait_ge(ld_w[2], layers)
                        part(key, BODY, fills, on_bank, t - start, parts)
            for t in TAIL:
                turn(t, (ITEMS - 1) * STEPS, (ITEMS - 1) * (STEPS // 2))
            for i in range(KT):
                values(0, i, ITEMS * (STEPS // 2), ITEMS * PAIRS)

            on_bank = [on_bank_before(k, ITEMS) for k in range(2)]
            pe.wait_ge(vec_in, ITEMS * PAIRS + 2)
            pe.wait_ge(ld_o, (L + 1) * 16 * LOADS_O + 16)
            for key in END:
                if key[0] == "h1":
                    pe.wait_ge(h1_ok, ITEMS + 1)
                if key[0] == "h2":
                    pe.wait_ge(h2_ok, ITEMS + 1)
                part(key, END, fills_before(ITEMS), on_bank)

            for k in range(2):
                pe.wait_ge(bank_in[k], on_bank_before(k, ITEMS) + END_ON[k])
            mod_rows(1)
            transpose_all(1)
            pe.wait_ge(tr_in, 2 * B)
            pe.wait_ge(ld_moe, 16 * 6)
            TILES = UNITS * FT
            with pe.Fori(0, B) as g:
                tiles = pe.snap(g * TILES)

                def hidden(u):
                    if u == 1:
                        pe.wait_ge(ld_ewo, 16 * (E + 1))
                    for f in range(FT):
                        j = u * FT + f
                        pe.wait_ge(er_ok, tiles + (j + 1))
                        w = GWI[:, f * P:(f + 1) * P] if u == 0 else EWI[:, u - 1, f * P:(f + 1) * P]
                        mm(FB[j % 4][:, :], w, HT[:, bass.ts(g, S)], start=True, stop=True).then_inc(e1_ok, 1)

                def second(u):
                    pe.wait_ge(eh_ok, tiles + ((u + 1) * FT + 4))
                    if u != 1:
                        pe.wait_ge(ey_ok, g * UNITS + max(u, 1))
                    for q in range(KT):
                        for f in range(FT):
                            w = GWO[:, f, :] if u == 0 else EWO[:, u - 1, f, :]
                            last = mm(PJ[u % 2][:, q * P:(q + 1) * P], HID[:, u % 2, f, q * P:(q + 1) * P], w,
                                      start=(f == 0), stop=(f == FT - 1))
                    last.then_inc(e2_ok, 1)

                hidden(0)
                for u in range(UNITS):
                    if u + 1 < UNITS:
                        hidden(u + 1)
                    second(u)


def kernel(**inputs):
    import concourse.bacc as _bacc
    from concourse.bass_utils import run_bass_kernel_spmd as _run

    a = {k: np.asarray(x) for k, x in inputs.items()}
    B, S, D = a["L0_attn_x"].shape
    L = a["L0_attn_W_qkv"].shape[0]
    FT = a["L0_attn_b_ff1"].shape[1] // P
    E = a["L0_ffn_exp_bi"].shape[0]
    pos = np.arange(S - 1, -1, -1, dtype=np.float32)
    freq = (np.float32(1.0) / np.float32(10000.0) ** (np.arange(0, D, 2, dtype=np.float32) / np.float32(D))).astype(np.float32)
    ang = (pos[:, None] * freq[None, :]).astype(np.float32)
    enc = np.concatenate([np.sin(ang), np.cos(ang)], axis=-1).astype(np.float32)
    g = lambda n: a["L0_" + n]
    arrays = [
        g("attn_x"), g("attn_W_qkv"), g("attn_W_r"), g("attn_W_o"),
        g("attn_u").reshape(-1, P).T, np.stack([g("attn_u").reshape(-1), g("attn_v").reshape(-1)]),
        g("attn_ln1_g"), g("attn_ln1_b"), g("attn_W_ff1"), g("attn_b_ff1").reshape(L, FT, P).transpose(0, 2, 1),
        g("attn_W_ff2"), g("attn_b_ff2"), g("attn_ln2_g"), g("attn_ln2_b"),
        g("ffn_gate_wi"), g("ffn_gate_bi").reshape(FT, P).T, g("ffn_gate_wo"), g("ffn_gate_bo"),
        g("ffn_exp_wi"), g("ffn_exp_bi").reshape(E, FT, P).transpose(2, 0, 1), g("ffn_exp_wo"), g("ffn_exp_bo"),
        g("c").T, g("wmod"), enc.T,
    ]
    nc = _bacc.Bacc("TRN2", target_bir_lowering=False, num_devices=1)
    sent, args = {}, []
    for i, x in enumerate(arrays):
        x = np.ascontiguousarray(x)
        sent[f"in_{i}"] = x
        args.append(nc.dram_tensor(f"in_{i}", x.shape, mybir.dt.from_np(x.dtype), kind="ExternalInput").ap())
    args.append(nc.dram_tensor("out", (B, S, D), F32, kind="ExternalOutput").ap())
    adaln_block(nc, *args)
    r = _run(nc, [sent], core_ids=[0])
    return r.results[0]["out"]
```
